# Optimizing a Trainium2 kernel written in Bass

```python
import numpy as np
import jax
import jax.numpy as jnp

def _softmax(x, axis=-1):
    return jax.nn.softmax(x, axis=axis)

def _gelu(x):
    return jax.nn.gelu(x, approximate=True)

def _silu(x):
    return jax.nn.silu(x)

def _sigmoid(x):
    return jax.nn.sigmoid(x)

def _layernorm(x, axis=-1, eps=1e-05):
    m = jnp.mean(x, axis=axis, keepdims=True)
    v = jnp.var(x, axis=axis, keepdims=True)
    return (x - m) / jnp.sqrt(v + eps)

def _scatter_add(tgt, idx, src, axis=0):
    return tgt.at[idx].add(src)

def _segment_sum(src, seg, n):
    return jax.ops.segment_sum(src, seg, n)
kernel_name = 'mk_xattn_ffn_d1_seqx_r8_e2d1ea'

def setup_inputs(seed: int=0):
    np.random.seed(seed)
    _w = jnp.asarray

    def _rec_inputs():
        import jax
        import jax.numpy as jnp
        _rk = jax.random.key(seed)
        x = -0.000125 + 0.9999 * jax.random.normal(jax.random.fold_in(_rk, 1), (4, 256, 128), jnp.float32)
        _lenS = 256 - jax.random.randint(jax.random.fold_in(_rk, 7), (4,), 0, max(1, 256 // 4) + 1, jnp.int32)
        _lenS2 = 1601 - jax.random.randint(jax.random.fold_in(_rk, 8), (4,), 0, max(1, 1601 // 4) + 1, jnp.int32)
        _ctx_768P = jax.random.normal(jax.random.fold_in(_rk, 11), (4, 16, 96), jnp.float32)
        _ctx_768c = jax.random.dirichlet(jax.random.fold_in(_rk, 511), 0.3 * jnp.ones((16,), jnp.float32), (4, 1601))
        _ctx_768t = jnp.einsum('bsk,bkd->bsd', _ctx_768c, _ctx_768P)
        _ctx_768t = _ctx_768t * jax.lax.rsqrt(jnp.mean(jnp.square(_ctx_768t)) + 1e-12) * 0.953939
        ctx_768 = 0.00272024 + 0.999456 * (_ctx_768t + 0.3 * jax.random.normal(jax.random.fold_in(_rk, 611), (4, 1601, 96), jnp.float32))
        return (x, ctx_768)
    x, ctx_768 = _rec_inputs()

    def _L0_xattn_setup():
        import jax, jax.numpy as jnp
        import numpy as np
        QUERY_DIM = 128
        CONTEXT_DIM = 96
        HEADS = 8
        DIM_HEAD = 64
        INNER = HEADS * DIM_HEAD
        key = jax.random.key(seed)
        ks = jax.random.split(key, 7)
        B, S, L = (8, 512, 77)
        x = jax.random.normal(ks[0], (B, S, QUERY_DIM), dtype=jnp.float32)
        context = jax.random.normal(ks[1], (B, L, CONTEXT_DIM), dtype=jnp.float32)
        Wq = jax.random.normal(ks[2], (QUERY_DIM, INNER), dtype=jnp.float32) * QUERY_DIM ** (-0.5)
        Wk = jax.random.normal(ks[3], (CONTEXT_DIM, INNER), dtype=jnp.float32) * CONTEXT_DIM ** (-0.5)
        Wv = jax.random.normal(ks[4], (CONTEXT_DIM, INNER), dtype=jnp.float32) * CONTEXT_DIM ** (-0.5)
        Wo = jax.random.normal(ks[5], (INNER, QUERY_DIM), dtype=jnp.float32) * INNER ** (-0.5)
        bo = jax.random.normal(ks[6], (QUERY_DIM,), dtype=jnp.float32) * 0.01
        return {'x': x, 'context': context, 'Wq': Wq, 'Wk': Wk, 'Wv': Wv, 'Wo': Wo, 'bo': bo}
    _L0_xattn_all = _L0_xattn_setup()
    _L0_xattn_in = {k: v for k, v in _L0_xattn_all.items() if k in ('Wq', 'Wk', 'Wv', 'Wo', 'bo')}
    del _L0_xattn_all

    def _L0_ffn_setup():
        import jax, jax.numpy as jnp
        import numpy as np
        D = 128
        H = 256
        E = 8
        TOP_K = 2
        N_SHARED = 1
        B, S = (2, 128)
        key = jax.random.key(seed)
        ks = jax.random.split(key, 12)
        sc = 0.02
        return {'hidden': jax.random.normal(ks[0], (B, S, D), jnp.float32), 'router_w': jax.random.normal(ks[1], (D, E), jnp.float32) * sc, 'router_b': jnp.zeros((E,), jnp.float32), 'sw1': jax.random.normal(ks[2], (D, H), jnp.float32) * sc, 'sb1': jnp.zeros((H,), jnp.float32), 'sw2': jax.random.normal(ks[3], (H, D), jnp.float32) * sc, 'sb2': jnp.zeros((D,), jnp.float32), 'rw1': jax.random.normal(ks[4], (E, D, H), jnp.float32) * sc, 'rb1': jnp.zeros((E, H), jnp.float32), 'rw2': jax.random.normal(ks[5], (E, H, D), jnp.float32) * sc, 'rb2': jnp.zeros((E, D), jnp.float32)}
    _L0_ffn_all = _L0_ffn_setup()
    _L0_ffn_in = {k: v for k, v in _L0_ffn_all.items() if k in ('router_w', 'router_b', 'sw1', 'sb1', 'sw2', 'sb2', 'rw1', 'rb1', 'rw2', 'rb2')}
    del _L0_ffn_all
    return {'x': x, 'ctx_768': ctx_768, 'L0_xattn_Wq': _L0_xattn_in['Wq'], 'L0_xattn_Wk': _L0_xattn_in['Wk'], 'L0_xattn_Wv': _L0_xattn_in['Wv'], 'L0_xattn_Wo': _L0_xattn_in['Wo'], 'L0_xattn_bo': _L0_xattn_in['bo'], 'L0_ffn_router_w': _L0_ffn_in['router_w'], 'L0_ffn_router_b': _L0_ffn_in['router_b'], 'L0_ffn_sw1': _L0_ffn_in['sw1'], 'L0_ffn_sb1': _L0_ffn_in['sb1'], 'L0_ffn_sw2': _L0_ffn_in['sw2'], 'L0_ffn_sb2': _L0_ffn_in['sb2'], 'L0_ffn_rw1': _L0_ffn_in['rw1'], 'L0_ffn_rb1': _L0_ffn_in['rb1'], 'L0_ffn_rw2': _L0_ffn_in['rw2'], 'L0_ffn_rb2': _L0_ffn_in['rb2']}

def reference(x, ctx_768, L0_xattn_Wq, L0_xattn_Wk, L0_xattn_Wv, L0_xattn_Wo, L0_xattn_bo, L0_ffn_router_w, L0_ffn_router_b, L0_ffn_sw1, L0_ffn_sb1, L0_ffn_sw2, L0_ffn_sb2, L0_ffn_rw1, L0_ffn_rb1, L0_ffn_rw2, L0_ffn_rb2):
    import jax
    import jax.numpy as jnp

    def _L0_xattn_ref(x, context, Wq, Wk, Wv, Wo, bo):
        import jax, jax.numpy as jnp
        import numpy as np
        QUERY_DIM = 128
        CONTEXT_DIM = 96
        HEADS = 8
        DIM_HEAD = 64
        INNER = HEADS * DIM_HEAD
        B, S, _ = x.shape
        L = context.shape[1]
        scale = DIM_HEAD ** (-0.5)
        q = (x @ Wq).reshape(B, S, HEADS, DIM_HEAD).transpose(0, 2, 1, 3)
        k = (context @ Wk).reshape(B, L, HEADS, DIM_HEAD).transpose(0, 2, 1, 3)
        v = (context @ Wv).reshape(B, L, HEADS, DIM_HEAD).transpose(0, 2, 1, 3)
        attn = jnp.einsum('bhsd,bhld->bhsl', q, k) * scale
        attn = jax.nn.softmax(attn, axis=-1)
        out = jnp.einsum('bhsl,bhld->bhsd', attn, v)
        out = out.transpose(0, 2, 1, 3).reshape(B, S, INNER)
        return out @ Wo + bo

    def _L0_ffn_ref(hidden, router_w, router_b, sw1, sb1, sw2, sb2, rw1, rb1, rw2, rb2):
        import jax, jax.numpy as jnp
        import numpy as np
        D = 128
        H = 256
        E = 8
        TOP_K = 2
        N_SHARED = 1
        B, S = (2, 128)
        b, s, d = hidden.shape
        T = b * s
        flat = hidden.reshape(T, d)
        router_logits = flat @ router_w + router_b
        router_probs = jax.nn.softmax(router_logits, axis=-1)
        topk_probs, topk_idx = jax.lax.top_k(router_probs, TOP_K)
        weights = jnp.zeros_like(router_probs).at[jnp.arange(T)[:, None], topk_idx].add(topk_probs)
        sh = jax.nn.gelu(flat @ sw1 + sb1, approximate=False)
        shared_out = (sh @ sw2 + sb2) / N_SHARED
        h1 = jax.nn.gelu(jnp.einsum('td,edh->teh', flat, rw1) + rb1[None], approximate=False)
        expert_out = jnp.einsum('teh,ehd->ted', h1, rw2) + rb2[None]
        mixed = jnp.einsum('ted,te->td', expert_out, weights)
        return (shared_out + mixed).reshape(b, s, d)
    x = x + _L0_xattn_ref(_layernorm(x, axis=-1), ctx_768, L0_xattn_Wq, L0_xattn_Wk, L0_xattn_Wv, L0_xattn_Wo, L0_xattn_bo)
    x = x + _L0_ffn_ref(_layernorm(x, axis=-1), L0_ffn_router_w, L0_ffn_router_b, L0_ffn_sw1, L0_ffn_sb1, L0_ffn_sw2, L0_ffn_sb2, L0_ffn_rw1, L0_ffn_rb1, L0_ffn_rw2, L0_ffn_rb2)
    return x

_drawn_inputs = setup_inputs


def setup_inputs(seed=0):
    import zlib

    import numpy as np

    out = dict(_drawn_inputs(seed))
    spreads = {'L0_ffn_router_b': (0.0, 0.77),
     'L0_ffn_sb1': (0.0, 0.575),
     'L0_ffn_sb2': (0.0, 0.1),
     'L0_ffn_rb1': (0.0, 0.8),
     'L0_ffn_rb2': (0.0, 0.393)}
    factors = {'L0_xattn_bo': 5.94, 'L0_ffn_router_w': 3.061, 'L0_ffn_rw1': 7.461, 'L0_ffn_rw2': 6.647}
    for name, (base, spread) in spreads.items():
        noise = np.random.default_rng([zlib.crc32(name.encode()), seed]).standard_normal(out[name].shape)
        drawn = base * np.exp(spread * noise) if base else spread * noise
        out[name] = jnp.asarray(drawn.astype(out[name].dtype))
    for name, factor in factors.items():
        out[name] = (out[name] * factor).astype(out[name].dtype)
    return out
```

```python
from contextlib import ExitStack

import concourse.bass as bass
from concourse import mybir

P = 128
ALU = mybir.AluOpType
ACT = mybir.ActivationFunctionType
F32 = mybir.dt.float32
F32R = mybir.dt.float32r
AX = mybir.AxisListType
LN_EPS = 1e-5


def key_units(chunks):
    return [list(range(c, min(c + 2, chunks))) for c in range(0, chunks, 2)]


def plan(batches, pairs, chunks, heads_per_pair, tiles, blocks):
    n_units = len(key_units(chunks))
    groups = (chunks + 3) // 4
    tasks = []
    for b in range(batches):
        tasks += [("turn", b, g) for g in range(groups)]
        for p in range(pairs):
            tasks.append(("g", b, p))
            tasks += [("max", b, p, i, t, k) for i in range(heads_per_pair) for t in range(tiles)
                      for k in range(blocks)]
            tasks.append(("shift", b, p))
    last_of = {t: n + 1 for n, t in enumerate(tasks)}
    per_batch = len(tasks) // batches
    start = last_of[("shift", 0, 0)]
    per_pair = pairs * n_units
    out, done, held = [], 0, None
    for b in range(batches):
        for p in range(pairs):
            for u in range(n_units):
                s = b * per_pair + p * n_units + u + 1
                want = round(start + (len(tasks) - start) * s / ((batches - 1) * per_pair))
                want = max(min(want, per_batch * (b + 2)), last_of[("shift", b, p)])
                while done < min(want, len(tasks)):
                    out.append(("ring", tasks[done]))
                    done += 1
                if p == 0:
                    out += [("ring", ("v", b, c)) for c in key_units(chunks)[u]]
                out.append(("scores", (b, p, u)))
                if held:
                    out.append(("values", held))
                held = (b, p, u)
                if u == 2 and (b, p) != (0, 0):
                    q = b * pairs + p - 1
                    out.append(("sums", (q // pairs, q % pairs)))
                    if q % pairs == pairs - 1:
                        out.append(("project", q // pairs))
    out += [("values", held), ("sums", (batches - 1, pairs - 1)), ("project", batches - 1)]
    return out


def build(nc, x, ctx_768, Wq, Wk, Wv, Wo, bo, router_w, router_b, sw1, sb1, sw2, sb2, rw1, rb1, rw2, rb2, out):
    B, S, D = x.shape
    L, C = ctx_768.shape[1:]
    INNER = Wq.shape[1]
    E, _, H = rw1.shape
    DH = 64
    HEADS = INNER // DH
    PAIRS = HEADS // 2
    T = S // P
    NT = B * T
    FULL = L // P
    REST = L - FULL * P
    CH = FULL + 1
    UNITS = key_units(CH)
    NU = len(UNITS)
    ROWC = C
    BLOCKS = 4
    BW = -(-L // BLOCKS)
    BW += BW % 2
    SCALE = float(DH) ** -0.5
    NE = E + 1
    HK = H // P
    HALF = 512
    NHALF = B * S // HALF
    TH = HALF // P
    WLO = 32
    assert D == P and 2 * DH == P and 0 < REST <= P and C + 1 <= P

    steps = plan(B, PAIRS, CH, 2, T, BLOCKS)
    ring_tasks = [w for kind, w in steps if kind == "ring"]
    ring_no, k = {}, 0
    for kind, w in steps:
        if kind == "ring":
            ring_no[w] = k
            k += 1
        if kind == "project":
            for what in ("y", "yt", "xt"):
                ring_no[(what, w)] = k
                k += 1

    def unit_no(b, p, u):
        return (b * PAIRS + p) * NU + u

    with ExitStack() as ctx:
        def sb(name, shape, dt=F32):
            return ctx.enter_context(nc.sbuf_tensor(name, shape, dt))

        def sem(name):
            return ctx.enter_context(nc.semaphore(name))

        ident = sb("ident", [P, P])
        x_sb = sb("x_sb", [P, NT, D])
        x1 = sb("x1", [P, NT, D])
        selectf = x1[:].rearrange("p a b -> p (a b)")[:, 0:E * P].rearrange("p (e q) -> p e q", e=E)
        xn = sb("xn", [P, NT, D])
        stats = sb("stats", [P, NT, 6])
        mv = sb("mv", [P, NT, 2])
        veps = sb("veps", [P, NT])
        rstd = sb("rstd", [P, NT])
        neg_half = sb("neg_half", [P, NT])
        xnT_hi = sb("xnT_hi", [P, B * S], F32R)
        xnT_lo = sb("xnT_lo", [P, B * S], F32R)
        ctx_raw = sb("ctx_raw", [P, 2, CH, C])
        ctxT_hi = sb("ctxT_hi", [C + 1, 2, L], F32R)
        ctxT_lo = sb("ctxT_lo", [C, 2, L], F32R)
        v_sb = sb("v_sb", [P, CH, INNER])
        g_hi = sb("g_hi", [C + 1, 2, HEADS, S], F32R)
        g_lo = sb("g_lo", [C, 2, HEADS, S], F32R)
        early = sb("early", [P, 2, INNER])
        wq_sb = early[:, 0, :]
        wk_sb = early[0:C, 1, :]
        wv_sb = sb("wv_sb", [C, INNER])
        wv_hi = sb("wv_hi", [C, INNER], F32R)
        wv_lo = sb("wv_lo", [C, INNER], F32R)
        wqT = sb("wqT", [P, PAIRS, D])
        wkT = sb("wkT", [P, PAIRS, C])
        m_all = sb("m", [D, 2, HEADS, C], F32R)
        m_hi, m_lo = m_all[:, 0], m_all[:, 1]
        wo_sb = sb("wo_sb", [P, PAIRS, D])
        maxes = sb("maxes", [P, 2, 2 * T, BLOCKS])
        neg_max = sb("neg_max", [P, 2, 2 * T, C + 1])
        probs = sb("probs", [P, 4, 2, 2 * S])
        work = sb("work", [P, 2, 2 * PAIRS * S])
        psum_keys = work[:, 0, :].rearrange("p (a b c) -> p a b c", a=2, b=2)
        ones = sb("ones", [P, DH])
        rden = sb("rden", [P, 2, S])
        oT = work[:, 1, :].rearrange("p (a b c) -> p a b c", a=2, b=PAIRS)
        yT = sb("yT", [P, S])
        bias_rows = sb("bias_rows", [NE * HK + 1, P])
        biasT = sb("biasT", [P, NE * HK + 1])
        w1_sb = work[:].rearrange("p a b -> p (a b)")[:, 0:NE * H].rearrange("p (e h) -> p e h", e=NE)
        w1_hi = sb("w1_hi", [D, NE, H], F32R)
        w1_lo = sb("w1_lo", [D, NE, H], F32R)
        w2_sb = sb("w2_sb", [P, NE, HK, D])
        rw_sb = sb("rw_sb", [D, E])
        rw_hi = sb("rw_hi", [D, E], F32R)
        rw_lo = sb("rw_lo", [D, E], F32R)
        rb_sb = sb("rb_sb", [P, E])
        b2_rows = sb("b2_rows", [P, D])
        select = sb("select", [P, E, P], F32R)
        before = sb("before", [P, E, E])
        logit = sb("logit", [P, NT, E])
        lmax = sb("lmax", [P, NT])
        lexp = sb("lexp", [P, NT, E])
        lsum = sb("lsum", [P, NT])
        rprob = sb("rprob", [P, NT, E])
        raw = ctx_raw[:].rearrange("p a b c -> p (a b c)")
        beats = raw[:, 0:NT * E * E].rearrange("p (t e j) -> p t e j", e=E, j=E)
        ties = raw[:, NT * E * E:2 * NT * E * E].rearrange("p (t e j) -> p t e j", e=E, j=E)
        rank = sb("rank", [P, NT, E])
        weight = sb("weight", [P, NT, E])
        wrow = early[:].rearrange("p a b -> p (a b)").rearrange("p (t r) -> p t r", t=NT)
        wT = m_all[:].rearrange("p a h c -> p (a h c)")[:, 0:B * S]
        w_hi = sb("w_hi", [P, NT, E], F32R)
        outT = xn[:].rearrange("p (h t) d -> p h (t d)", h=NHALF)
        out_sb = x_sb
        hid = probs[:, 0:2, :, :].rearrange("p a b c -> p (a b) c")
        hid_w = probs[:, 2:4, :, :].rearrange("p a b c -> p (a b) c")

        ps = ctx.enter_context(nc.psum_tensor("ps", [P, 8, 512], F32))

        def s_bank(n, c):
            return ps[:, 2 * (n % 2) + c, :]

        def ring(k):
            return ps[:, 4 + k % 2, :]

        def o_bank(pair):
            return ps[:, 6 + pair % 2, :]

        s_wqk, s_x, s_wv = sem("loaded_wqk"), sem("loaded_x"), sem("loaded_wv")
        s_ctx = [sem(f"loaded_ctx{b}") for b in range(B)]
        s_wo, s_bias, s_w1, s_w2 = sem("loaded_wo"), sem("loaded_bias"), sem("loaded_w1"), sem("loaded_w2")
        s_rw, s_b2 = sem("loaded_router"), sem("loaded_b2")
        pool_done = sem("pool_done")
        consts_ready = sem("consts_ready")
        w_split = sem("w_split")
        rstd_ready = sem("rstd_ready")
        var_ready = sem("var_ready")
        dve_done = sem("dve_done")
        setup_filled = sem("setup_filled")
        setup_taken = sem("setup_taken")
        xn_ready = sem("xn_ready")
        ring_filled = sem("ring_filled")
        ring_taken = sem("ring_taken")
        max_ready = sem("max_ready")
        scores_ready = sem("scores_ready")
        probs_ready = sem("probs_ready")
        values_done = sem("values_done")
        summed = sem("summed")
        sums_ready = sem("sums_ready")
        o_ready = sem("o_ready")
        o_taken = sem("o_taken")
        router_filled, router_taken = sem("router_filled"), sem("router_taken")
        logit_ready, lexp_ready, w_ready = sem("logit_ready"), sem("lexp_ready"), sem("w_ready")
        wt_filled, wt_taken = sem("wt_filled"), sem("wt_taken")
        bcast_ready, bcast_used = sem("bcast_ready"), sem("bcast_used")
        h_ready, hid_ready, hidw_ready = sem("h_ready"), sem("hid_ready"), sem("hidw_ready")
        w2_done = sem("w2_done")
        outT_taken = sem("outT_taken")
        back_filled, out_ready, s_out = sem("back_filled"), sem("out_ready"), sem("stored")

        block = ctx.enter_context(nc.Block())
        items = [(h, e, k) for h in range(NHALF) for e in [E] + list(range(E)) for k in range(HK)]
        NI = len(items)

        @block.sync
        def _(sp):
            sp.dma_start(wq_sb[:], Wq).then_inc(s_wqk, 16)
            sp.dma_start(wk_sb[:], Wk).then_inc(s_wqk, 16)
            for b in range(B):
                if b >= 2:
                    sp.wait_ge(ring_taken, ring_no[("turn", b - 2, (CH + 3) // 4 - 1)] + 1)
                sp.dma_start(ctx_raw[:, b % 2, 0:FULL, :],
                             ctx_768[b, 0:FULL * P].rearrange("(p j) d -> p j d", j=FULL)).then_inc(s_ctx[b], 16)
                sp.dma_start(ctx_raw[0:REST, b % 2, FULL, :], ctx_768[b, FULL * P:L]).then_inc(s_ctx[b], 16)
                if b == 0:
                    sp.dma_start(wv_sb[:], Wv).then_inc(s_wv, 16)
                if b == 1:
                    sp.dma_start(wo_sb[:], Wo.rearrange("(c p) d -> p c d", p=P)).then_inc(s_wo, 16)
                    sp.dma_start(w2_sb[:, 0:E], rw2.rearrange("e (k p) d -> p e k d", p=P)).then_inc(s_w2, 16)
                    sp.dma_start(w2_sb[:, E], sw2.rearrange("(k p) d -> p k d", p=P)).then_inc(s_w2, 16)
            for h in range(NHALF):
                sp.wait_ge(out_ready, h + 1)
                bb = HALF // S
                sp.dma_start(out[h * bb:(h + 1) * bb].rearrange("b (p j) d -> p b (j d)", j=T),
                             out_sb[:, h * TH:(h + 1) * TH, :].rearrange("p (b j) d -> p b (j d)", j=T)
                             ).then_inc(s_out, 16)
            sp.wait_ge(s_out, 16 * NHALF)

        @block.gpsimd
        def _(pool):
            g = nc.gpsimd
            n = 0
            for ap, value in ((ident, 0.0), (neg_max, 0.0), (ones, 1.0), (selectf, 0.0), (b2_rows, 0.0),
                              (before, 1.0), (neg_half, -0.5)):
                g.memset(ap if ap is selectf else ap[:], value).then_inc(pool_done, 1)
                n += 1
            pool.wait_ge(pool_done, n)
            g.affine_select(out=ident[:], in_=ident[:], compare_op=ALU.not_equal, fill=1.0, base=0,
                            pattern=[[-1, P]], channel_multiplier=1).then_inc(consts_ready, 1)
            for n_sel, base in enumerate((0, -WLO)):
                g.affine_select(out=selectf, in_=selectf, compare_op=ALU.not_equal, fill=1.0, base=base,
                                pattern=[[-1, E], [0, P]], channel_multiplier=1).then_inc(pool_done, 1)
                n += 1
                pool.wait_ge(pool_done, n)
            g.tensor_copy(select[:], selectf).then_inc(consts_ready, 1)
            g.affine_select(out=before[:], in_=before[:], compare_op=ALU.is_gt, fill=0.0, base=0,
                            pattern=[[1, E], [-1, E]], channel_multiplier=0).then_inc(consts_ready, 1)
            pool.wait_ge(var_ready, 1)
            g.tensor_tensor(rstd[:], veps[:], neg_half[:], ALU.pow).then_inc(rstd_ready, 1)
            pool.wait_ge(s_wv, 16)
            g.tensor_copy(wv_hi[:], wv_sb[:]).then_inc(pool_done, 1)
            pool.wait_ge(pool_done, n + 1)
            g.tensor_tensor(wv_lo[:], wv_sb[:], wv_hi[:].bitcast(F32), ALU.subtract).then_inc(w_split, 1)
            pool.wait_ge(s_w1, 32)
            pool.wait_ge(s_rw, 32)
            g.tensor_copy(w1_hi[:], w1_sb[:]).then_inc(pool_done, 1)
            g.tensor_copy(rw_hi[:], rw_sb[:]).then_inc(pool_done, 1)
            pool.wait_ge(pool_done, n + 3)
            g.tensor_tensor(w1_lo[:], w1_sb[:], w1_hi[:].bitcast(F32), ALU.subtract).then_inc(w_split, 1)
            g.tensor_tensor(rw_lo[:], rw_sb[:], rw_hi[:].bitcast(F32), ALU.subtract).then_inc(w_split, 1)
            done = [n + 3]

            def then_own(ins):
                done[0] += 1
                ins.then_inc(pool_done, 1)
                pool.wait_ge(pool_done, done[0])

            pool.wait_ge(w_split, 3)
            for kind, w in steps:
                if kind == "project":
                    pool.wait_ge(var_ready, w + 2)
                    t = slice(w * T, w * T + T)
                    g.tensor_tensor(rstd[:, t], veps[:, t], neg_half[:, t], ALU.pow).then_inc(rstd_ready, 1)
                if kind != "scores":
                    continue
                b, p, u = w
                n, pair = unit_no(*w), b * PAIRS + p
                acc = psum_keys[:, pair % 2]
                pool.wait_ge(probs_ready, n + 1)
                pr = probs[:, n % 4]
                if u == 0:
                    continue
                if u == 1:
                    if pair >= 2:
                        pool.wait_ge(o_ready, pair - 1)
                    g.tensor_tensor(acc, probs[:, (n - 1) % 4], pr, ALU.add).then_inc(summed, 1)
                elif u < NU - 1:
                    g.tensor_tensor(acc, acc, pr, ALU.add).then_inc(summed, 1)
                pool.wait_ge(summed, pair * (NU - 1) + min(u, NU - 2) + 0)
                if u == NU - 1:
                    then_own(g.tensor_tensor(acc[:, 0], acc[:, 0], acc[:, 1], ALU.add))
                    g.tensor_tensor(acc[0:REST, 0], acc[0:REST, 0], pr[0:REST, 0], ALU.add).then_inc(summed, 1)

        @block.scalar
        def _(act):
            act.dma_start(x_sb[:].rearrange("p (b j) d -> p b (j d)", j=T),
                          x.rearrange("b (p j) d -> p b (j d)", j=T)).then_inc(s_x, 16)
            act.dma_start(bias_rows[0:E * HK], rb1.rearrange("e (k p) -> (e k) p", p=P)).then_inc(s_bias, 16)
            act.dma_start(bias_rows[E * HK:NE * HK], sb1.rearrange("(k p) -> k p", p=P)).then_inc(s_bias, 16)
            act.dma_start(bias_rows[NE * HK:NE * HK + 1], bo.rearrange("(k p) -> k p", p=P)).then_inc(s_bias, 16)
            act.dma_start(w1_sb[:, 0:E], rw1.rearrange("e d h -> d e h")).then_inc(s_w1, 16)
            act.dma_start(w1_sb[:, E], sw1).then_inc(s_w1, 16)
            act.dma_start(rw_sb[:], router_w).then_inc(s_rw, 16)
            act.dma_start(rb_sb[:], router_b.rearrange("(o e) -> o e", o=1).to_broadcast([P, E])).then_inc(s_rw, 16)
            act.wait_ge(pool_done, 7)
            act.dma_start(b2_rows[0:E], rb2).then_inc(s_b2, 16)
            act.dma_start(b2_rows[WLO:WLO + E], rb2).then_inc(s_b2, 16)
            act.dma_start(b2_rows[E:E + 1], sb2.rearrange("(o d) -> o d", o=1)).then_inc(s_b2, 16)
            for kind, w in steps:
                if kind != "scores":
                    continue
                n, u = unit_no(*w), w[2]
                act.wait_ge(scores_ready, n + 1)
                if n >= 4:
                    act.wait_ge(values_done, n - 3)
                    pair, uu = (n - 4) // NU, (n - 4) % NU
                    act.wait_ge(summed, pair * (NU - 1) + max(uu, 1))
                wide = len(UNITS[u])
                rows = P if wide == 2 else REST
                s = ps[0:rows, 2 * (n % 2):2 * (n % 2) + wide, :]
                nc.scalar.activation(probs[0:rows, n % 4, 0:wide, :], s, ACT.Exp,
                                     scale=SCALE).then_inc(probs_ready, 1)
            act.wait_ge(logit_ready, 1)
            nc.scalar.activation(lexp[:], logit[:], ACT.Exp).then_inc(lexp_ready, 1)
            for n, (h, e, k) in enumerate(items):
                act.wait_ge(h_ready, n + 1)
                if n >= 4:
                    if items[n - 4][1] == E:
                        act.wait_ge(w2_done, n - 3)
                    else:
                        act.wait_ge(hidw_ready, n - 3)
                c = e * HK + k
                nc.scalar.activation(hid[:, n % 4, :], ps[:, n % 4, :], ACT.Gelu,
                                     bias=biasT[:, c:c + 1]).then_inc(hid_ready, 1)

        @block.vector
        def _(dve):
            v = nc.vector
            count = [0]

            def then_own(ins):
                count[0] += 1
                ins.then_inc(dve_done, 1)
                dve.wait_ge(dve_done, count[0])

            def halves(hi, lo, src, signal):
                then_own(v.tensor_copy(hi, src))
                v.tensor_tensor(lo, src, hi.bitcast(F32), ALU.subtract).then_inc(signal, 1)

            def moments(src, tiles):
                for t in tiles:
                    ins = v.bn_stats(stats[:, t, :], src[:, t, :])
                then_own(ins)
                for t in tiles:
                    ins = v.bn_aggr(mv[:, t, :], stats[:, t, :])
                then_own(ins)
                ts = slice(tiles[0], tiles[-1] + 1)
                v.tensor_scalar(veps[:, ts], mv[:, ts, 1], LN_EPS, None, ALU.add).then_inc(var_ready, 1)

            def normal(src, tiles, round_no):
                dve.wait_ge(rstd_ready, round_no)
                for t in tiles:
                    ins = v.tensor_scalar(xn[:, t, :], src[:, t, :], mv[:, t, 0:1], rstd[:, t:t + 1],
                                          ALU.subtract, ALU.mult)
                ins.then_inc(xn_ready, 1)

            then_own(v.memset(ctxT_hi[C:C + 1, :, :].bitcast(F32), 1.0))
            dve.wait_ge(setup_filled, 1)
            v.tensor_copy(wqT[:], ps[:, 0, :].rearrange("p (c d) -> p c d", c=PAIRS)).then_inc(setup_taken, 1)
            dve.wait_ge(setup_filled, 2)
            v.tensor_copy(wkT[:], ps[:, 1, 0:PAIRS * C].rearrange("p (c d) -> p c d", c=PAIRS)
                          ).then_inc(setup_taken, 1)
            dve.wait_ge(s_x, 16)
            dve.wait_ge(pool_done, 7)
            moments(x_sb, range(NT))
            for i in range(2):
                dve.wait_ge(setup_filled, 3 + i)
                hs = slice(i, HEADS, 2)
                halves(m_hi[:, hs, :], m_lo[:, hs, :],
                       ps[:, 2 + i, 0:PAIRS * C].rearrange("p (h c) -> p h c", h=PAIRS), setup_taken)
            normal(x_sb, range(NT), 1)
            for i in range(2):
                dve.wait_ge(setup_filled, 5 + i)
                cs = slice(i * 512, (i + 1) * 512)
                halves(xnT_hi[:, cs], xnT_lo[:, cs], ps[:, 4 + i, :], setup_taken)
            dve.wait_ge(setup_filled, 7)
            v.tensor_copy(biasT[:], ps[:, 6, 0:NE * HK + 1]).then_inc(setup_taken, 1)

            for kind, w in steps:
                if kind == "ring":
                    k = ring_no[w]
                    src = ring(k)
                    dve.wait_ge(ring_filled, k + 1)
                    b = w[1]
                    if w[0] == "turn":
                        c0 = 4 * w[2] * P
                        c1 = min(c0 + 4 * P, L)
                        if w[2] == 0 and b >= 2:
                            dve.wait_ge(scores_ready, unit_no(b - 2, PAIRS - 1, NU - 1) + 1)
                        halves(ctxT_hi[0:C, b % 2, c0:c1], ctxT_lo[:, b % 2, c0:c1], src[0:C, 0:c1 - c0], ring_taken)
                    elif w[0] == "g":
                        hs = slice(2 * w[2], 2 * w[2] + 2)
                        gv = src[0:C, :].rearrange("p (h s) -> p h s", h=2)
                        halves(g_hi[0:C, b % 2, hs, :], g_lo[:, b % 2, hs, :], gv, ring_taken)
                    elif w[0] == "v":
                        c = w[2]
                        rows = P if c < FULL else REST
                        if b >= 1:
                            dve.wait_ge(values_done, unit_no(b - 1, PAIRS - 1, c // 2) + 1)
                        v.tensor_copy(v_sb[0:rows, c, :], src[0:rows, :]).then_inc(ring_taken, 1)
                    elif w[0] == "max":
                        _, b, p, i, t, blk = w
                        v.tensor_reduce(maxes[:, p % 2, i * T + t, blk:blk + 1], src[:, 0:BW], AX.X,
                                        ALU.max).then_inc(ring_taken, 1)
                        if (i, t, blk) == (1, T - 1, BLOCKS - 1):
                            dve.wait_ge(ring_taken, k + 1)
                            v.tensor_reduce(neg_max[:, p % 2, :, C], maxes[:, p % 2, :, :], AX.X, ALU.max,
                                            negate=True).then_inc(max_ready, 1)
                    elif w[0] == "shift":
                        p = w[2]
                        v.tensor_copy(g_hi[C:C + 1, b % 2, 2 * p:2 * p + 2, :],
                                      src[C:C + 1, :].rearrange("p (h s) -> p h s", h=2)).then_inc(ring_taken, 1)
                elif kind == "sums":
                    b, p = w
                    pair = b * PAIRS + p
                    dve.wait_ge(o_ready, pair + 1)
                    then_own(v.reciprocal(rden[:, pair % 2, :], o_bank(pair)[:, S:2 * S]))
                    v.tensor_tensor(oT[:, b % 2, p, :], o_bank(pair)[:, 0:S], rden[:, pair % 2, :],
                                    ALU.mult).then_inc(o_taken, 1)
                elif kind == "project":
                    b = w
                    tiles = range(b * T, (b + 1) * T)
                    k = ring_no[("y", b)]
                    dve.wait_ge(ring_filled, k + 1)
                    v.tensor_scalar(yT[:], ring(k)[:, 0:S], biasT[:, NE * HK:NE * HK + 1], None,
                                    ALU.add).then_inc(ring_taken, 1)
                    k = ring_no[("yt", b)]
                    dve.wait_ge(ring_filled, k + 1)
                    v.tensor_tensor(x1[:, b * T:(b + 1) * T, :],
                                    ring(k)[:, 0:T * D].rearrange("p (t d) -> p t d", t=T),
                                    x_sb[:, b * T:(b + 1) * T, :], ALU.add).then_inc(ring_taken, 1)
                    dve.wait_ge(ring_taken, k + 1)
                    moments(x1, tiles)
                    normal(x1, tiles, b + 2)
                    k = ring_no[("xt", b)]
                    dve.wait_ge(ring_filled, k + 1)
                    halves(xnT_hi[:, b * S:(b + 1) * S], xnT_lo[:, b * S:(b + 1) * S], ring(k)[:, 0:S], ring_taken)

            then_own(v.memset(wrow, 0.0))
            dve.wait_ge(router_filled, 1)
            dve.wait_ge(s_rw, 32)
            then_own(v.tensor_tensor(logit[:], ps[:, 4, 0:NT * E].rearrange("p (t e) -> p t e", e=E),
                                     rb_sb[:].unsqueeze(1).to_broadcast([P, NT, E]), ALU.add))
            then_own(v.tensor_reduce(lmax[:], logit[:], AX.X, ALU.max))
            v.tensor_tensor(logit[:], logit[:], lmax[:].unsqueeze(2).to_broadcast([P, NT, E]),
                            ALU.subtract).then_inc(logit_ready, 1)
            dve.wait_ge(lexp_ready, 1)
            then_own(v.tensor_reduce(lsum[:], lexp[:], AX.X, ALU.add))
            then_own(v.reciprocal(lsum[:], lsum[:]))
            then_own(v.tensor_tensor(rprob[:], lexp[:], lsum[:].unsqueeze(2).to_broadcast([P, NT, E]), ALU.mult))
            dve.wait_ge(consts_ready, 3)
            for t in range(NT):
                of_j = rprob[:, t, :].unsqueeze(1).to_broadcast([P, E, E])
                of_e = rprob[:, t, :].unsqueeze(2).to_broadcast([P, E, E])
                v.tensor_tensor(beats[:, t], of_j, of_e, ALU.is_gt)
                ins = v.tensor_tensor(ties[:, t], of_j, of_e, ALU.is_equal)
            then_own(ins)
            then_own(v.tensor_tensor(ties[:], ties[:], before[:].unsqueeze(1).to_broadcast([P, NT, E, E]), ALU.mult))
            then_own(v.tensor_tensor(beats[:], beats[:], ties[:], ALU.add))
            then_own(v.tensor_reduce(rank[:], beats[:], AX.X, ALU.add))
            then_own(v.scalar_tensor_tensor(weight[:], rank[:], 2.0, rprob[:], ALU.is_lt, ALU.mult))
            then_own(v.tensor_copy(w_hi[:], weight[:]))
            hi = w_hi[:].bitcast(F32)
            v.tensor_copy(wrow[:, :, 0:E], hi)
            v.tensor_tensor(wrow[:, :, WLO:WLO + E], weight[:], hi, ALU.subtract)
            v.memset(wrow[:, :, E:E + 1], 1.0).then_inc(w_ready, 1)
            for i in range(NHALF):
                dve.wait_ge(wt_filled, i + 1)
                v.tensor_copy(wT[:, i * HALF:(i + 1) * HALF], ps[:, 4 + i % 2, :]).then_inc(wt_taken, 1)

            nb = 0
            for n, (h, e, k) in enumerate(items):
                if e < E:
                    dve.wait_ge(hid_ready, n + 1)
                    if n >= 4:
                        dve.wait_ge(w2_done, n - 3)
                    if k == 0:
                        nb += 1
                        dve.wait_ge(bcast_ready, nb)
                    ins = v.tensor_tensor(hid_w[:, n % 4, :], ps[:, 4 + (nb - 1) % 2, :], hid[:, n % 4, :], ALU.mult)
                    ins.then_inc(hidw_ready, 1)
                else:
                    dve.wait_ge(hid_ready, n + 1)
                    v.memset(hid_w[0:1, n % 4, 0:1], 0.0).then_inc(hidw_ready, 1)
                if n % (NI // NHALF) == NI // NHALF - 1:
                    h_no = h
                    dve.wait_ge(w2_done, n + 1)
                    v.tensor_copy(outT[:, h_no, :], ps[:, 6 + h_no % 2, :]).then_inc(outT_taken, 1)
                    dve.wait_ge(back_filled, h_no + 1)
                    v.tensor_tensor(out_sb[:, h_no * TH:(h_no + 1) * TH, :],
                                    ps[:, 6 + h_no % 2, :].rearrange("p (t d) -> p t d", t=TH),
                                    x1[:, h_no * TH:(h_no + 1) * TH, :], ALU.add).then_inc(out_ready, 1)

        @block.tensor
        def _(pe):
            mm, turn = nc.tensor.matmul, nc.tensor.transpose
            idr = ident[:]

            def three(dst, a_hi, a_lo, b_hi, b_lo, start=True, stop=True):
                mm(dst, a_hi, b_hi, start=start, stop=False)
                mm(dst, a_hi, b_lo, start=False, stop=False)
                return mm(dst, a_lo, b_hi, start=False, stop=stop)

            pe.wait_ge(consts_ready, 1)
            pe.wait_ge(s_wqk, 32)
            for c in range(PAIRS):
                ins = turn(ps[:, 0, c * D:(c + 1) * D], wq_sb[:, c * P:(c + 1) * P], idr)
            ins.then_inc(setup_filled, 1)
            for c in range(PAIRS):
                ins = turn(ps[:, 1, c * C:(c + 1) * C], wk_sb[:, c * P:(c + 1) * P], idr[0:C, 0:C])
            ins.then_inc(setup_filled, 1)
            pe.wait_ge(setup_taken, 2)
            for h in range(HEADS):
                r = DH * (h % 2)
                ins = mm(ps[:, 2 + h % 2, (h // 2) * C:(h // 2 + 1) * C], wqT[r:r + DH, h // 2, :],
                         wkT[r:r + DH, h // 2, :], start=True, stop=True)
                if h >= HEADS - 2:
                    ins.then_inc(setup_filled, 1)
            pe.wait_ge(xn_ready, 1)
            for t in range(NT):
                ins = turn(ps[:, 4 + t // 4, (t % 4) * P:(t % 4 + 1) * P], xn[:, t, :], idr)
                if t % 4 == 3:
                    ins.then_inc(setup_filled, 1)
            pe.wait_ge(s_bias, 48)
            nb = NE * HK + 1
            turn(ps[:, 6, 0:nb], bias_rows[:, :], idr[0:nb, 0:nb]).then_inc(setup_filled, 1)
            pe.wait_ge(setup_taken, 7)

            def ring_free(k):
                if k >= 2:
                    pe.wait_ge(ring_taken, k - 1)

            for kind, w in steps:
                if kind == "ring":
                    k = ring_no[w]
                    dst = ring(k)
                    b = w[1]
                    ring_free(k)
                    if w[0] == "turn":
                        if w[2] == 0:
                            pe.wait_ge(s_ctx[b], 32)
                        for c in range(4 * w[2], min(4 * w[2] + 4, CH)):
                            rows = P if c < FULL else REST
                            j = c - 4 * w[2]
                            ins = turn(dst[0:C, j * P:j * P + rows], ctx_raw[0:rows, b % 2, c, :],
                                       idr[0:rows, 0:rows])
                    elif w[0] == "g":
                        for i in range(2):
                            h = 2 * w[2] + i
                            q = slice(b * S, (b + 1) * S)
                            ins = three(dst[0:C, i * S:(i + 1) * S], m_hi[:, h, :], m_lo[:, h, :],
                                        xnT_hi[:, q], xnT_lo[:, q])
                    elif w[0] == "v":
                        c = w[2]
                        rows = P if c < FULL else REST
                        pe.wait_ge(w_split, 1)
                        pe.wait_ge(ring_taken, ring_no[("turn", b, c // 4)] + 1)
                        ks = slice(c * P, c * P + rows)
                        ins = three(dst[0:rows, :], ctxT_hi[0:C, b % 2, ks], ctxT_lo[:, b % 2, ks], wv_hi[:], wv_lo[:])
                    elif w[0] == "max":
                        _, b, p, i, t, blk = w
                        pe.wait_ge(ring_taken, ring_no[("g", b, p)] + 1)
                        k0 = min(blk * BW, L - BW)
                        ins = mm(dst[:, 0:BW], g_hi[0:C, b % 2, 2 * p + i, t * P:(t + 1) * P],
                                 ctxT_hi[0:C, b % 2, k0:k0 + BW], start=True, stop=True)
                    elif w[0] == "shift":
                        p = w[2]
                        pe.wait_ge(max_ready, b * PAIRS + p + 1)
                        for j in range(2 * T):
                            ins = turn(dst[0:C + 1, j * P:(j + 1) * P], neg_max[:, p % 2, j, :], idr)
                    ins.then_inc(ring_filled, 1)
                elif kind == "scores":
                    b, p, u = w
                    n = unit_no(*w)
                    pe.wait_ge(ring_taken, ring_no[("shift", b, p)] + 1)
                    if n >= 2:
                        pe.wait_ge(probs_ready, n - 1)
                    for j, c in enumerate(UNITS[u]):
                        rows = P if c < FULL else REST
                        ks = slice(c * P, c * P + rows)
                        dst = s_bank(n, j)[0:rows, :]
                        gh = g_hi[:, b % 2, 2 * p:2 * p + 2, :].rearrange("p h s -> p (h s)")
                        gl = g_lo[:, b % 2, 2 * p:2 * p + 2, :].rearrange("p h s -> p (h s)")
                        mm(dst, ctxT_hi[:, b % 2, ks], gh, start=True, stop=False)
                        mm(dst, ctxT_hi[0:C, b % 2, ks], gl, start=False, stop=False)
                        ins = mm(dst, ctxT_lo[:, b % 2, ks], gh[0:C], start=False, stop=True)
                    ins.then_inc(scores_ready, 1)
                elif kind == "values":
                    b, p, u = w
                    n, pair = unit_no(*w), b * PAIRS + p
                    pe.wait_ge(probs_ready, n + 1)
                    if u == 0 and pair >= 2:
                        pe.wait_ge(o_taken, pair - 1)
                    for j, c in enumerate(UNITS[u]):
                        rows = P if c < FULL else REST
                        if p == 0:
                            pe.wait_ge(ring_taken, ring_no[("v", b, c)] + 1)
                        for i in range(2):
                            h = 2 * p + i
                            ins = mm(o_bank(pair)[DH * i:DH * (i + 1), 0:S], v_sb[0:rows, c, h * DH:(h + 1) * DH],
                                     probs[0:rows, n % 4, j, i * S:(i + 1) * S], start=(c == 0), stop=(c == CH - 1))
                    ins.then_inc(values_done, 1)
                elif kind == "sums":
                    b, p = w
                    pair = b * PAIRS + p
                    pe.wait_ge(summed, (pair + 1) * (NU - 1))
                    for i in range(2):
                        ins = mm(o_bank(pair)[DH * i:DH * (i + 1), S:2 * S], ones[:, :],
                                 psum_keys[:, pair % 2, 0, i * S:(i + 1) * S], start=True, stop=True)
                    ins.then_inc(o_ready, 1)
                elif kind == "project":
                    b = w
                    k = ring_no[("y", b)]
                    ring_free(k)
                    pe.wait_ge(o_taken, (b + 1) * PAIRS)
                    pe.wait_ge(s_wo, 16)
                    for c in range(PAIRS):
                        ins = mm(ring(k)[:, 0:S], wo_sb[:, c, :], oT[:, b % 2, c, :], start=(c == 0),
                                 stop=(c == PAIRS - 1))
                    ins.then_inc(ring_filled, 1)
                    k = ring_no[("yt", b)]
                    ring_free(k)
                    pe.wait_ge(ring_taken, ring_no[("y", b)] + 1)
                    for t in range(T):
                        ins = turn(ring(k)[:, t * D:(t + 1) * D], yT[:, t * P:(t + 1) * P], idr)
                    ins.then_inc(ring_filled, 1)
                    k = ring_no[("xt", b)]
                    ring_free(k)
                    pe.wait_ge(xn_ready, b + 2)
                    for t in range(T):
                        ins = turn(ring(k)[:, t * P:(t + 1) * P], xn[:, b * T + t, :], idr)
                    ins.then_inc(ring_filled, 1)

            last_ring = max(ring_no.values()) + 1
            pe.wait_ge(ring_taken, last_ring)
            pe.wait_ge(w_split, 3)
            for t in range(NT):
                q = slice(t * P, (t + 1) * P)
                ins = three(ps[:, 4, t * E:(t + 1) * E], xnT_hi[:, q], xnT_lo[:, q], rw_hi[:], rw_lo[:])
            ins.then_inc(router_filled, 1)

            def first(n):
                h, e, k = items[n]
                if n >= 4:
                    pe.wait_ge(hid_ready, n - 3)
                q = slice(h * HALF, (h + 1) * HALF)
                ks = slice(k * P, (k + 1) * P)
                three(ps[:, n % 4, :], w1_hi[:, e, ks], w1_lo[:, e, ks], xnT_hi[:, q], xnT_lo[:, q]
                      ).then_inc(h_ready, 1)

            def weight_rows():
                pe.wait_ge(w_ready, 1)
                for i in range(NHALF):
                    for t in range(TH):
                        ins = turn(ps[:, 4 + i % 2, t * P:(t + 1) * P], wrow[:, i * TH + t, :], idr)
                    ins.then_inc(wt_filled, 1)
                pe.wait_ge(s_b2, 48)

            sent = [0]

            def spread(h, e):
                nb = sent[0]
                if nb < 2:
                    pe.wait_ge(wt_taken, NHALF)
                if nb >= 2:
                    pe.wait_ge(hidw_ready, last_use[nb - 2] + 1)
                mm(ps[:, 4 + nb % 2, :], select[:, e, :], wT[:, h * HALF:(h + 1) * HALF], start=True,
                   stop=True).then_inc(bcast_ready, 1)
                sent[0] += 1

            last_use = [n for n, (h, e, k) in enumerate(items) if e < E and k == HK - 1]

            def second(n):
                h, e, k = items[n]
                per = NI // NHALF
                if n % per == 0:
                    pe.wait_ge(wt_taken, NHALF)
                    mm(ps[:, 6 + h % 2, :], b2_rows[:], wT[:, h * HALF:(h + 1) * HALF].bitcast(F32), start=True,
                       stop=False)
                pe.wait_ge(hidw_ready, n + 1)
                src = hid if e == E else hid_w
                ins = mm(ps[:, 6 + h % 2, :], w2_sb[:, e, k, :], src[:, n % 4, :], start=False,
                         stop=(n % per == per - 1))
                ins.then_inc(w2_done, 1)
                if n % per == per - 1:
                    pe.wait_ge(outT_taken, h + 1)
                    for t in range(TH):
                        ins = turn(ps[:, 6 + h % 2, t * P:(t + 1) * P], outT[:, h, t * P:(t + 1) * P], idr)
                    ins.then_inc(back_filled, 1)

            LAG = 2
            pe.wait_ge(s_w2, 32)
            for n in range(NI + LAG):
                if n < NI:
                    first(n)
                    if n == 1:
                        weight_rows()
                    h, e, k = items[n]
                    if e < E and k == 0:
                        spread(h, e)
                if n >= LAG:
                    second(n - LAG)


_INS = ["x", "ctx_768", "L0_xattn_Wq", "L0_xattn_Wk", "L0_xattn_Wv", "L0_xattn_Wo", "L0_xattn_bo",
        "L0_ffn_router_w", "L0_ffn_router_b", "L0_ffn_sw1", "L0_ffn_sb1", "L0_ffn_sw2", "L0_ffn_sb2",
        "L0_ffn_rw1", "L0_ffn_rb1", "L0_ffn_rw2", "L0_ffn_rb2"]


def kernel(**inputs):
    import numpy as _np
    import concourse.bacc as _bacc
    from concourse import mybir as _mybir
    from concourse.bass_utils import run_bass_kernel_spmd as _run

    nc = _bacc.Bacc("TRN2", target_bir_lowering=False, num_devices=1)
    arrays, args = {}, []
    for name in _INS:
        a = _np.ascontiguousarray(inputs[name])
        arrays[f"in_{name}_dram"] = a
        args.append(nc.dram_tensor(f"in_{name}_dram", a.shape, _mybir.dt.from_np(a.dtype), kind="ExternalInput").ap())
    shape = inputs["x"].shape
    out = nc.dram_tensor("out_0_dram", shape, _mybir.dt.from_np(_np.dtype("float32")), kind="ExternalOutput").ap()
    build(nc, *args, out)
    r = _run(nc, [arrays], core_ids=[0])
    return r.results[0]["out_0_dram"]
```

```python
from contextlib import ExitStack

import concourse.bass as bass
from concourse import mybir

P = 128
TOP = 2
RING = 3
LEAD = 1.6
ALU = mybir.AluOpType
ACT = mybir.ActivationFunctionType
F32 = mybir.dt.float32
F32R = mybir.dt.float32r
AX = mybir.AxisListType
LN_EPS = 1e-5


def key_units(chunks):
    return [list(range(c, min(c + 2, chunks))) for c in range(0, chunks, 2)]


COST = {"max": 1.0, "v": 1.2, "turn": 2.4, "g": 2.4, "shift": 1.2, "y": 1.0, "yt": 4.0, "xt": 1.5, "sums": 4.5,
        "router": 2.0, "wrow": 1.0, "v0": 0.0, "stats": 2.0, "normal": 1.0,
        "xn": 2.4, "rank": 5.0}


def plan(batches, pairs, chunks, heads_per_pair, tiles, blocks, halves):
    units = key_units(chunks)
    n_units = len(units)
    turns = [("turn", b, g) for b in range(batches) for g in range((chunks + 3) // 4)]
    per_batch = len(turns) // batches
    order = [(b, p) for b in range(batches) for p in range(pairs)]
    tasks = turns[:per_batch] + [("g", 0, 0)]
    n_v0 = 0
    late = []
    for n, (b, p) in enumerate(order):
        maxima = [("max", b, p, i, t, k) for i in range(heads_per_pair) for t in range(tiles)
                  for k in range(blocks)]
        put = dict(late)
        if n == 1:
            put.update({1: ("stats", 1), 3: ("stats", 2), 5: ("normal", 1), 6: ("stats", 3), 8: ("normal", 2),
                        10: ("xn", 0), 11: ("normal", 3), 14: ("xn", 1)})
        if n + 1 < len(order):
            nb, np_ = order[n + 1]
            if np_ == 0:
                for g in range(per_batch):
                    put[5 + 2 * g] = turns[nb * per_batch + g]
            put[len(maxima) - 3] = ("g", nb, np_)
        for m, task in enumerate(maxima):
            tasks.append(task)
            if n == 0 and n_v0 < chunks:
                tasks.append(("v0", n_v0))
                n_v0 += 1
            if m in put:
                tasks.append(put[m])
        late = [(2, ("shift", b, p))]
        if n == 0 or n + 1 == len(order):
            tasks.append(("shift", b, p))
            late = []
    last_of = {t: n + 1 for n, t in enumerate(tasks)}
    start = last_of[("shift", 0, 0)]
    main, held = [], []
    for b, p in order:
        q = order[order.index((b, p)) - 1] if (b, p) != (0, 0) else None
        for u, unit in enumerate(units):
            for j, c in enumerate(unit):
                if p == 0 and b:
                    main.append(("ring", ("v", b, c)))
                main.append(("scores", (b, p, u, j)))
            main += held
            held = [("values", (b, p, u, j)) for j in range(len(unit))]
            if q and u == 0:
                main.append(("take", q))
            if q and u == 2:
                main.append(("ring", ("sums",) + q))
            if q and q[1] == pairs - 1 and u in (4, 5):
                main.append(("ring", (("y", "yt")[u - 4], q[0])))
            if q and q[1] == 0 and q[0] and u == 0:
                main.append(("ring", ("xt", q[0] - 1)))
            if q and q[1] == 0 and q[0] and q[0] % (batches // halves) == 0:
                h = q[0] * halves // batches - 1
                if u in (3, 4, 6):
                    main.append({3: ("ring", ("router", h)), 4: ("rank", h), 6: ("ring", ("wrow", h))}[u])
    main += held + [("take", order[-1])]

    def cost(x):
        return COST[x[1][0]] if x[0] == "ring" else COST.get(x[0], 0.0)

    steps = sum(kind in ("scores", "values") for kind, _ in main)
    spread = steps * (batches * pairs - LEAD) / (batches * pairs)
    total = sum(COST[t[0]] for t in tasks[start:]) + sum(cost(x) for x in main)
    def event(task):
        return (task[0], task[1]) if task[0] in ("v0", "stats", "normal") else ("ring", task)

    out, done, step, spent = [event(t) for t in tasks[:start]], start, 0, 0.0
    for x in main:
        kind, w = x
        if kind in ("scores", "values"):
            step += 1
        if kind == "scores" or kind == "values" and w[3] == 0:
            need = last_of[("shift", w[0], w[1])] if kind == "scores" else 0
            while done < len(tasks) and (done < need or spent + COST[tasks[done][0]] / 2 < total * step / spread):
                out.append(event(tasks[done]))
                spent += COST[tasks[done][0]]
                done += 1
        out.append(x)
        spent += cost(x)
    return out


def plan_experts(experts, chunks, halves, last_pair):
    b = last_pair[0]
    between = {0: [("ring", ("sums",) + last_pair)],
               1: [("ring", ("y", b))], 2: [("ring", ("yt", b))], 4: [("ring", ("xt", b))],
               5: [("ring", ("router", halves - 1))], 6: [("rank", halves - 1)],
               7: [("ring", ("wrow", halves - 1))]}
    out, n, done = [], 0, []
    for h in range(halves):
        for turn, e in enumerate([experts] + list(range(experts))):
            if e < experts:
                out.append(("ring", ("spread", h, e)))
            new = list(range(n, n + chunks))
            out += [("first", i) for i in new]
            out += [("weigh", i) for i in new if e < experts]
            out += [("second", i) for i in done]
            if h and turn == 0:
                out.append(("out", h - 1))
            if h and turn == 1:
                out.append(("back", h - 1))
            if h == 0:
                out += between.get(turn, [])
            done, n = new, n + chunks
    return out + [("second", i) for i in done] + [("out", halves - 1), ("back", halves - 1)]


def build(nc, x, ctx_768, Wq, Wk, Wv, Wo, bo, router_w, router_b, sw1, sb1, sw2, sb2, rw1, rb1, rw2, rb2, out):
    B, S, D = x.shape
    L, C = ctx_768.shape[1:]
    INNER = Wq.shape[1]
    E, _, H = rw1.shape
    DH = 64
    HEADS = INNER // DH
    PAIRS = HEADS // 2
    T = S // P
    NT = B * T
    FULL = L // P
    REST = L - FULL * P
    CH = FULL + 1
    UNITS = key_units(CH)
    NU = len(UNITS)
    ROWC = C
    BLOCKS = 4
    BW = -(-L // BLOCKS)
    BW += BW % 2
    SCALE = float(DH) ** -0.5
    NE = E + 1
    HK = H // P
    HALF = 512
    NHALF = B * S // HALF
    TH = HALF // P
    WLO = 32
    assert D == P and 2 * DH == P and 0 < REST <= P and C + 1 <= P

    steps = plan(B, PAIRS, CH, 2, T, BLOCKS, NHALF) + plan_experts(E, HK, NHALF, (B - 1, PAIRS - 1))
    ring_no = {w: k for k, w in enumerate(w for kind, w in steps if kind == "ring")}

    def turn_columns(g):
        return 4 * g * P, min(4 * g * P + 4 * P, L)

    def unit_no(b, p, u):
        return (b * PAIRS + p) * NU + u

    with ExitStack() as ctx:
        def sb(name, shape, dt=F32):
            return ctx.enter_context(nc.sbuf_tensor(name, shape, dt))

        def sem(name):
            return ctx.enter_context(nc.semaphore(name))

        ident = sb("ident", [P, P])
        x_sb = sb("x_sb", [P, NT, D])
        x1 = sb("x1", [P, NT, D])
        xn = sb("xn", [P, NT, D])
        stats = sb("stats", [P, NT, 6])
        mv = sb("mv", [P, NT, 2])
        veps = sb("veps", [P, NT])
        rstd = sb("rstd", [P, NT])
        neg_half = sb("neg_half", [P, NT])
        xnT_hi = sb("xnT_hi", [P, B * S], F32R)
        xnT_lo = sb("xnT_lo", [P, B * S], F32R)
        ctx_raw = sb("ctx_raw", [P, 2, CH, C])
        ctxT_hi = sb("ctxT_hi", [C + 1, 2, L], F32R)
        ctxT_lo = sb("ctxT_lo", [C, 2, L], F32R)
        v_sb = sb("v_sb", [P, CH, INNER])
        g_hi = sb("g_hi", [C + 1, 2, HEADS, S], F32R)
        g_lo = sb("g_lo", [C, 2, HEADS, S], F32R)
        early = sb("early", [P, 2, INNER])
        wq_sb = early[:, 0, :]
        wk_sb = early[0:C, 1, :]
        wv_hi = sb("wv_hi", [C, INNER], F32R)
        wv_lo = sb("wv_lo", [C, INNER], F32R)
        m_all = sb("m", [D, 2, HEADS, C], F32R)
        m_hi, m_lo = m_all[:, 0], m_all[:, 1]
        wo_sb = sb("wo_sb", [P, PAIRS, D])
        maxes = sb("maxes", [P, 2, 2 * T, BLOCKS])
        neg_max = sb("neg_max", [P, 2, 2 * T, C + 1])
        probs = sb("probs", [P, 4, 2, 2 * S])
        wv_sb = probs[0:C, 2, 0, :]
        wqT = probs[:, 3, 0, :].rearrange("p (c d) -> p c d", c=PAIRS)
        wkT = probs[:, 3, 1, 0:PAIRS * C].rearrange("p (c d) -> p c d", c=PAIRS)
        work = sb("work", [P, 2, 2 * PAIRS * S])
        psum_keys = work[:, 0, :].rearrange("p (a b c) -> p a b c", a=2, b=2)
        ones = sb("ones", [P, DH])
        rden = sb("rden", [P, S])
        o_raw = sb("o_raw", [P, S])
        oT = work[:, 1, :].rearrange("p (a b c) -> p a b c", a=2, b=PAIRS)
        yT = sb("yT", [P, S])
        freed = sb("freed", [1, 1])
        bias_rows = sb("bias_rows", [NE * HK + 1, P])
        biasT = sb("biasT", [P, NE * HK + 1])
        w1_sb = work[:].rearrange("p a b -> p (a b)")[:, 0:NE * H].rearrange("p (e h) -> p e h", e=NE)
        w1_hi = sb("w1_hi", [D, NE, H], F32R)
        w1_lo = sb("w1_lo", [D, NE, H], F32R)
        w2_sb = sb("w2_sb", [P, NE, HK, D])
        rw_sb = sb("rw_sb", [D, E])
        rw_hi = sb("rw_hi", [D, E], F32R)
        rw_lo = sb("rw_lo", [D, E], F32R)
        rb_sb = sb("rb_sb", [P, E])
        b2_rows = sb("b2_rows", [P, D])
        select = sb("select", [P, E], F32R)
        selectf = sb("selectf", [P, E])
        before = sb("before", [P, E, E])
        logit = sb("logit", [P, TH, E])
        lmax = sb("lmax", [P, TH])
        lexp = sb("lexp", [P, TH, E])
        lsum = sb("lsum", [P, TH])
        rsum = sb("rsum", [P, TH])
        rprob = sb("rprob", [P, TH, E])
        beats = sb("beats", [P, TH, E, E])
        ties = sb("ties", [P, TH, E, E])
        rank = sb("rank", [P, TH, E])
        weight = sb("weight", [P, TH, E])
        wrow = early[:].rearrange("p a b -> p (a b)").rearrange("p (t r) -> p t r", t=NT)
        wT = sb("wT", [P, B * S], F32R)
        w_hi = sb("w_hi", [P, TH, E], F32R)
        outT = xn[:].rearrange("p (h t) d -> p h (t d)", h=NHALF)
        out_sb = x_sb
        hid = probs[:, 0:2, :, :].rearrange("p a b c -> p (a b) c")
        hid_w = probs[:, 2:4, :, :].rearrange("p a b c -> p (a b) c")

        ps = ctx.enter_context(nc.psum_tensor("ps", [P, 8, 512], F32))

        def s_bank(n, c):
            return ps[:, 2 * (n % 2) + c, :]

        def ring(k):
            return ps[:, 4 + k % RING, :]

        o_bank = ps[:, 4 + RING, 0:S]
        HB = 3

        def out_bank(h):
            return ps[:, (7, 3)[h % 2], :]

        s_wqk, s_x0, s_x, s_wv = sem("loaded_wqk"), sem("loaded_x0"), sem("loaded_x"), sem("loaded_wv")
        s_ctx = [sem(f"loaded_ctx{b}") for b in range(B)]
        s_wo, s_bias, s_w1, s_w2 = sem("loaded_wo"), sem("loaded_bias"), sem("loaded_w1"), sem("loaded_w2")
        s_rw, s_b2 = sem("loaded_router"), sem("loaded_b2")
        pool_done = sem("pool_done")
        consts_ready = sem("consts_ready")
        w_split = sem("w_split")
        rstd_ready = sem("rstd_ready")
        var_ready = sem("var_ready")
        dve_done = sem("dve_done")
        setup_filled = sem("setup_filled")
        setup_taken = sem("setup_taken")
        xn_ready = sem("xn_ready")
        s_bias_turned = sem("bias_turned")
        ring_filled = sem("ring_filled")
        ring_taken = sem("ring_taken")
        max_ready = sem("max_ready")
        scores_ready = sem("scores_ready")
        probs_ready = sem("probs_ready")
        values_done = sem("values_done")
        summed = sem("summed")
        sums_ready = sem("sums_ready")
        o_raw_ready = sem("o_raw_ready")
        o_taken = sem("o_taken")
        v0_filled, v0_taken = sem("v0_filled"), sem("v0_taken")
        first_ready = sem("first_ready")
        turn_hi = sem("turn_hi")
        logit_ready, lexp_ready, w_ready = sem("logit_ready"), sem("lexp_ready"), sem("w_ready")
        h_ready, hid_ready, hidw_ready = sem("h_ready"), sem("hid_ready"), sem("hidw_ready")
        w2_done = sem("w2_done")
        outT_taken = sem("outT_taken")
        back_filled, out_ready, s_out = sem("back_filled"), sem("out_ready"), sem("stored")

        block = ctx.enter_context(nc.Block())
        items = [(h, e, k) for h in range(NHALF) for e in [E] + list(range(E)) for k in range(HK)]
        NI = len(items)
        weighed, count = {}, 0
        for n, (h, e, k) in enumerate(items):
            count += e < E
            weighed[n] = count
        LAST_UNIT = B * PAIRS * NU
        assert (LAST_UNIT - 1) % 4 == 3

        @block.sync
        def _(sp):
            sp.dma_start(wq_sb[:], Wq).then_inc(s_wqk, 16)
            sp.dma_start(wk_sb[:], Wk).then_inc(s_wqk, 16)
            for b in range(B):
                if b >= 2:
                    sp.wait_ge(ring_taken, ring_no[("turn", b - 2, (CH + 3) // 4 - 1)] + 1)
                sp.dma_start(ctx_raw[:, b % 2, 0:FULL, :],
                             ctx_768[b, 0:FULL * P].rearrange("(p j) d -> p j d", j=FULL)).then_inc(s_ctx[b], 16)
                sp.dma_start(ctx_raw[0:REST, b % 2, FULL, :], ctx_768[b, FULL * P:L]).then_inc(s_ctx[b], 16)
                if b == 0:
                    sp.dma_start(wv_sb, Wv).then_inc(s_wv, 16)
                    sp.dma_start(w1_sb[:, 0:E], rw1.rearrange("e d h -> d e h")).then_inc(s_w1, 16)
                    sp.dma_start(w1_sb[:, E], sw1).then_inc(s_w1, 16)
                    sp.dma_start(rw_sb[:], router_w).then_inc(s_rw, 16)
                    sp.dma_start(rb_sb[:], router_b.rearrange("(o e) -> o e", o=1).to_broadcast([P, E])
                                 ).then_inc(s_rw, 16)
                    sp.dma_start(bias_rows[0:E * HK], rb1.rearrange("e (k p) -> (e k) p", p=P)).then_inc(s_bias, 16)
                    sp.dma_start(bias_rows[E * HK:NE * HK], sb1.rearrange("(k p) -> k p", p=P)).then_inc(s_bias, 16)
                    sp.dma_start(bias_rows[NE * HK:NE * HK + 1], bo.rearrange("(k p) -> k p", p=P)
                                 ).then_inc(s_bias, 16)
                if b == 1:
                    sp.dma_start(wo_sb[:], Wo.rearrange("(c p) d -> p c d", p=P)).then_inc(s_wo, 16)
                    sp.dma_start(w2_sb[:, 0:E], rw2.rearrange("e (k p) d -> p e k d", p=P)).then_inc(s_w2, 16)
                    sp.dma_start(w2_sb[:, E], sw2.rearrange("(k p) d -> p k d", p=P)).then_inc(s_w2, 16)
                    sp.wait_ge(pool_done, 3)
                    sp.dma_start(b2_rows[0:E], rb2).then_inc(s_b2, 16)
                    sp.dma_start(b2_rows[WLO:WLO + E], rb2).then_inc(s_b2, 16)
                    sp.dma_start(b2_rows[E:E + 1], sb2.rearrange("(o d) -> o d", o=1)).then_inc(s_b2, 16)
            for h in range(NHALF):
                sp.wait_ge(out_ready, h + 1)
                bb = HALF // S
                sp.dma_start(out[h * bb:(h + 1) * bb].rearrange("b (p j) d -> p b (j d)", j=T),
                             out_sb[:, h * TH:(h + 1) * TH, :].rearrange("p (b j) d -> p b (j d)", j=T)
                             ).then_inc(s_out, 16)
            sp.wait_ge(s_out, 16 * NHALF)

        @block.gpsimd
        def _(pool):
            g = nc.gpsimd
            done = [0]

            def own(ins):
                done[0] += 1
                ins.then_inc(pool_done, 1)

            def then_own(ins):
                own(ins)
                pool.wait_ge(pool_done, done[0])

            def inverse_roots(tiles, round_no):
                pool.wait_ge(var_ready, round_no)
                g.tensor_tensor(rstd[:, tiles], veps[:, tiles], neg_half[:, tiles], ALU.pow).then_inc(rstd_ready, 1)

            own(g.memset(neg_half[:], -0.5))
            then_own(g.memset(ident[:], 0.0))
            g.affine_select(out=ident[:], in_=ident[:], compare_op=ALU.not_equal, fill=1.0, base=0,
                            pattern=[[-1, P]], channel_multiplier=1).then_inc(consts_ready, 1)
            for ap, value in ((b2_rows, 0.0), (neg_max, 0.0), (ones, 1.0), (selectf, 0.0)):
                own(g.memset(ap[:], value))
            then_own(g.memset(before[:], 1.0))
            inverse_roots(slice(0, T), 1)
            pool.wait_ge(s_wv, 16)
            then_own(g.tensor_copy(wv_hi[:], wv_sb))
            g.tensor_tensor(wv_lo[:], wv_sb, wv_hi[:].bitcast(F32), ALU.subtract).then_inc(w_split, 1)
            for base in (0, -WLO):
                then_own(g.affine_select(out=selectf[:], in_=selectf[:], compare_op=ALU.not_equal, fill=1.0,
                                         base=base, pattern=[[-1, E]], channel_multiplier=1))
            g.tensor_copy(select[:], selectf[:]).then_inc(consts_ready, 1)
            g.affine_select(out=before[:], in_=before[:], compare_op=ALU.is_gt, fill=0.0, base=0,
                            pattern=[[1, E], [-1, E]], channel_multiplier=0).then_inc(consts_ready, 1)
            pool.wait_ge(consts_ready, 3)
            g.memset(ctxT_hi[C:C + 1, :, :].bitcast(F32), 1.0).then_inc(consts_ready, 1)
            pool.wait_ge(consts_ready, 4)
            pool.wait_ge(s_w1, 32)
            pool.wait_ge(s_rw, 32)
            own(g.tensor_copy(w1_hi[:], w1_sb))
            then_own(g.tensor_copy(rw_hi[:], rw_sb[:]))
            g.tensor_tensor(w1_lo[:], w1_sb, w1_hi[:].bitcast(F32), ALU.subtract).then_inc(w_split, 1)
            g.tensor_tensor(rw_lo[:], rw_sb[:], rw_hi[:].bitcast(F32), ALU.subtract).then_inc(w_split, 1)

            pool.wait_ge(w_split, 3)
            for kind, w in steps:
                if kind == "stats":
                    inverse_roots(slice(w * T, w * T + T), w + 1)
                if kind == "ring" and w[0] == "yt":
                    inverse_roots(slice(w[1] * T, w[1] * T + T), B + w[1] + 1)
                if kind != "scores" or w[3]:
                    continue
                b, p, u, _ = w
                n, pair = unit_no(b, p, u), b * PAIRS + p
                acc = psum_keys[:, pair % 2]
                pool.wait_ge(probs_ready, n + 1)
                pr = probs[:, n % 4]
                if u == 0:
                    continue
                if u == 1:
                    if pair >= 2:
                        pool.wait_ge(ring_filled, ring_no[("sums",) + divmod(pair - 2, PAIRS)] + 1)
                    g.tensor_tensor(acc, probs[:, (n - 1) % 4], pr, ALU.add).then_inc(summed, 1)
                elif u < NU - 1:
                    g.tensor_tensor(acc, acc, pr, ALU.add).then_inc(summed, 1)
                pool.wait_ge(summed, pair * (NU - 1) + min(u, NU - 2) + 0)
                if u == NU - 1:
                    then_own(g.tensor_tensor(acc[:, 0], acc[:, 0], acc[:, 1], ALU.add))
                    g.tensor_tensor(acc[0:REST, 0], acc[0:REST, 0], pr[0:REST, 0], ALU.add).then_inc(summed, 1)

        @block.scalar
        def _(act):
            xv = x_sb[:].rearrange("p (b j) d -> p b (j d)", j=T)
            xd = x.rearrange("b (p j) d -> p b (j d)", j=T)
            act.dma_start(xv[:, 0:1], xd[:, 0:1]).then_inc(s_x0, 16)
            act.dma_start(xv[:, 1:B], xd[:, 1:B]).then_inc(s_x, 16)
            act.wait_ge(setup_filled, 1)
            nc.scalar.copy(wqT, ps[:, 0, :].rearrange("p (c d) -> p c d", c=PAIRS)).then_inc(first_ready, 1)
            act.wait_ge(setup_filled, 2)
            nc.scalar.copy(wkT, ps[:, 1, 0:PAIRS * C].rearrange("p (c d) -> p c d", c=PAIRS)
                           ).then_inc(first_ready, 1)
            for kind, w in steps:
                if kind == "ring" and w[0] == "turn" and w[1] == 0:
                    act.wait_ge(ring_filled, ring_no[w] + 1)
                    c0, c1 = turn_columns(w[2])
                    nc.scalar.copy(ctxT_hi[0:C, 0, c0:c1], ring(ring_no[w])[0:C, 0:c1 - c0]).then_inc(turn_hi, 1)
                elif kind == "v0":
                    rows = P if w < FULL else REST
                    act.wait_ge(v0_filled, w + 1)
                    nc.scalar.copy(v_sb[0:rows, w, :], ps[0:rows, w % 4, :]).then_inc(v0_taken, 1)
                elif kind == "scores" and w[3] == 0:
                    n, u = unit_no(*w[:3]), w[2]
                    act.wait_ge(scores_ready, n + 1)
                    if n == 2:
                        act.wait_ge(w_split, 1)
                    if n >= 4:
                        act.wait_ge(values_done, n - 3)
                        pair, uu = (n - 4) // NU, (n - 4) % NU
                        act.wait_ge(summed, pair * (NU - 1) + max(uu, 1))
                    wide = len(UNITS[u])
                    rows = P if wide == 2 else REST
                    s = ps[0:rows, 2 * (n % 2):2 * (n % 2) + wide, :]
                    nc.scalar.activation(probs[0:rows, n % 4, 0:wide, :], s, ACT.Exp,
                                         scale=SCALE).then_inc(probs_ready, 1)
                elif kind == "take":
                    pair = w[0] * PAIRS + w[1]
                    act.wait_ge(values_done, NU * (pair + 1))
                    if pair:
                        act.wait_ge(o_taken, pair)
                    nc.scalar.copy(o_raw[:], o_bank).then_inc(o_raw_ready, 1)
                elif kind == "ring" and w[0] == "router":
                    act.wait_ge(logit_ready, w[1] + 1)
                    nc.scalar.activation(lexp[:], logit[:], ACT.Exp).then_inc(lexp_ready, 1)
                elif kind == "first":
                    n, e, k = w, items[w][1], items[w][2]
                    act.wait_ge(h_ready, n + 1)
                    if n == 0:
                        act.wait_ge(s_bias_turned, 1)
                        act.wait_ge(values_done, LAST_UNIT - 1)
                        act.wait_ge(summed, B * PAIRS * (NU - 1) - 2)
                    if n >= 4:
                        if items[n - 4][1] == E:
                            act.wait_ge(w2_done, n - 3)
                        else:
                            act.wait_ge(hidw_ready, weighed[n - 4])
                    c = e * HK + k
                    nc.scalar.activation(hid[:, n % 4, :], ps[:, n % HB, :], ACT.Gelu,
                                         bias=biasT[:, c:c + 1]).then_inc(hid_ready, 1)

        @block.vector
        def _(dve):
            v = nc.vector
            count = [0]

            def then_own(ins):
                count[0] += 1
                ins.then_inc(dve_done, 1)
                dve.wait_ge(dve_done, count[0])

            def halves(hi, lo, src, signal):
                then_own(v.tensor_copy(hi, src))
                v.tensor_tensor(lo, src, hi.bitcast(F32), ALU.subtract).then_inc(signal, 1)

            def moments(src, tiles):
                for t in tiles:
                    ins = v.bn_stats(stats[:, t, :], src[:, t, :])
                then_own(ins)
                for t in tiles:
                    ins = v.bn_aggr(mv[:, t, :], stats[:, t, :])
                then_own(ins)
                ts = slice(tiles[0], tiles[-1] + 1)
                v.tensor_scalar(veps[:, ts], mv[:, ts, 1], LN_EPS, None, ALU.add).then_inc(var_ready, 1)

            def normal(src, tiles, round_no):
                dve.wait_ge(rstd_ready, round_no)
                for t in tiles:
                    ins = v.tensor_scalar(xn[:, t, :], src[:, t, :], mv[:, t, 0:1], rstd[:, t:t + 1],
                                          ALU.subtract, ALU.mult)
                ins.then_inc(xn_ready, 1)

            dve.wait_ge(s_x0, 16)
            moments(x_sb, range(T))
            normal(x_sb, range(T), 1)
            for i in range(2):
                dve.wait_ge(setup_filled, 3 + i)
                hs = slice(i, HEADS, 2)
                halves(m_hi[:, hs, :], m_lo[:, hs, :],
                       ps[:, 2 + i, 0:PAIRS * C].rearrange("p (h c) -> p h c", h=PAIRS), setup_taken)
            dve.wait_ge(setup_filled, 5)
            halves(xnT_hi[:, 0:S], xnT_lo[:, 0:S], ps[:, 7, 0:S], setup_taken)

            for kind, w in steps:
                if kind == "ring":
                    k = ring_no[w]
                    src = ring(k)
                    dve.wait_ge(ring_filled, k + 1)
                    b = w[1]
                    if w[0] == "xn":
                        t0 = T + 4 * b
                        t1 = min(t0 + 4, NT)
                        if b == 1:
                            v.tensor_copy(biasT[:], src[:, P * (t1 - t0):P * (t1 - t0) + NE * HK + 1]
                                          ).then_inc(s_bias_turned, 1)
                        halves(xnT_hi[:, t0 * P:t1 * P], xnT_lo[:, t0 * P:t1 * P], src[:, 0:(t1 - t0) * P], ring_taken)
                    elif w[0] == "turn":
                        c0, c1 = turn_columns(w[2])
                        if w[2] == 0 and b >= 2:
                            dve.wait_ge(scores_ready, unit_no(b - 2, PAIRS - 1, NU - 1) + 1)
                        if b == 0:
                            dve.wait_ge(turn_hi, w[2] + 1)
                            v.tensor_tensor(ctxT_lo[:, 0, c0:c1], src[0:C, 0:c1 - c0],
                                            ctxT_hi[0:C, 0, c0:c1].bitcast(F32), ALU.subtract
                                            ).then_inc(ring_taken, 1)
                            continue
                        halves(ctxT_hi[0:C, b % 2, c0:c1], ctxT_lo[:, b % 2, c0:c1], src[0:C, 0:c1 - c0], ring_taken)
                    elif w[0] == "g":
                        hs = slice(2 * w[2], 2 * w[2] + 2)
                        gv = src[0:C, :].rearrange("p (h s) -> p h s", h=2)
                        halves(g_hi[0:C, b % 2, hs, :], g_lo[:, b % 2, hs, :], gv, ring_taken)
                    elif w[0] == "v":
                        c = w[2]
                        rows = P if c < FULL else REST
                        if b >= 1:
                            dve.wait_ge(values_done, unit_no(b - 1, PAIRS - 1, c // 2) + 1)
                        v.tensor_copy(v_sb[0:rows, c, :], src[0:rows, :]).then_inc(ring_taken, 1)
                    elif w[0] == "max":
                        _, b, p, i, t, blk = w
                        v.tensor_reduce(maxes[:, p % 2, i * T + t, blk:blk + 1], src[:, 0:BW], AX.X,
                                        ALU.max).then_inc(ring_taken, 1)
                        if (i, t, blk) == (1, T - 1, BLOCKS - 1):
                            dve.wait_ge(ring_taken, k + 1)
                            v.tensor_reduce(neg_max[:, p % 2, :, C], maxes[:, p % 2, :, :], AX.X, ALU.max,
                                            negate=True).then_inc(max_ready, 1)
                    elif w[0] == "shift":
                        p = w[2]
                        v.tensor_copy(g_hi[C:C + 1, b % 2, 2 * p:2 * p + 2, :],
                                      src[C:C + 1, :].rearrange("p (h s) -> p h s", h=2)).then_inc(ring_taken, 1)
                    elif w[0] == "sums":
                        pair = b * PAIRS + w[2]
                        if pair:
                            dve.wait_ge(o_taken, pair)
                        v.reciprocal(rden[:], src[:, 0:S]).then_inc(ring_taken, 1)
                        dve.wait_ge(ring_taken, k + 1)
                        dve.wait_ge(o_raw_ready, pair + 1)
                        v.tensor_tensor(oT[:, b % 2, w[2], :], o_raw[:], rden[:], ALU.mult).then_inc(o_taken, 1)
                    elif w[0] == "y":
                        v.tensor_scalar(yT[:], src[:, 0:S], biasT[:, NE * HK:NE * HK + 1], None,
                                        ALU.add).then_inc(ring_taken, 1)
                    elif w[0] == "yt":
                        tiles = range(b * T, (b + 1) * T)
                        v.tensor_tensor(x1[:, b * T:(b + 1) * T, :], src[:, 0:T * D].rearrange("p (t d) -> p t d", t=T),
                                        x_sb[:, b * T:(b + 1) * T, :], ALU.add).then_inc(ring_taken, 1)
                        dve.wait_ge(ring_taken, k + 1)
                        moments(x1, tiles)
                        normal(x1, tiles, B + b + 1)
                    elif w[0] == "xt":
                        halves(xnT_hi[:, b * S:(b + 1) * S], xnT_lo[:, b * S:(b + 1) * S], src[:, 0:S], ring_taken)
                    elif w[0] == "router":
                        if b == 0:
                            dve.wait_ge(s_rw, 32)
                            then_own(v.memset(wrow, 0.0))
                        then_own(v.tensor_tensor(logit[:], src[:, 0:TH * E].rearrange("p (t e) -> p t e", e=E),
                                                 rb_sb[:].unsqueeze(1).to_broadcast([P, TH, E]), ALU.add))
                        then_own(v.tensor_reduce(lmax[:], logit[:], AX.X, ALU.max))
                        v.tensor_tensor(logit[:], logit[:], lmax[:].unsqueeze(2).to_broadcast([P, TH, E]),
                                        ALU.subtract).then_inc(logit_ready, 1)
                        dve.wait_ge(logit_ready, b + 1)
                        v.memset(freed[:], 0.0).then_inc(ring_taken, 1)
                    elif w[0] == "wrow":
                        v.tensor_copy(wT[:, b * HALF:(b + 1) * HALF], src).then_inc(ring_taken, 1)
                elif kind == "rank":
                    dve.wait_ge(lexp_ready, w + 1)
                    then_own(v.tensor_reduce(lsum[:], lexp[:], AX.X, ALU.add))
                    then_own(v.reciprocal(rsum[:], lsum[:]))
                    then_own(v.tensor_tensor(rprob[:], lexp[:], rsum[:].unsqueeze(2).to_broadcast([P, TH, E]),
                                             ALU.mult))
                    dve.wait_ge(consts_ready, 3)
                    for t in range(TH):
                        of_j = rprob[:, t, :].unsqueeze(1).to_broadcast([P, E, E])
                        of_e = rprob[:, t, :].unsqueeze(2).to_broadcast([P, E, E])
                        v.tensor_tensor(beats[:, t], of_j, of_e, ALU.is_gt)
                        ins = v.tensor_tensor(ties[:, t], of_j, of_e, ALU.is_equal)
                    then_own(ins)
                    then_own(v.tensor_tensor(ties[:], ties[:], before[:].unsqueeze(1).to_broadcast([P, TH, E, E]),
                                             ALU.mult))
                    then_own(v.tensor_tensor(beats[:], beats[:], ties[:], ALU.add))
                    then_own(v.tensor_reduce(rank[:], beats[:], AX.X, ALU.add))
                    then_own(v.scalar_tensor_tensor(weight[:], rank[:], float(TOP), rprob[:], ALU.is_lt, ALU.mult))
                    then_own(v.tensor_copy(w_hi[:], weight[:]))
                    hi = w_hi[:].bitcast(F32)
                    wr = wrow[:, w * TH:(w + 1) * TH, :]
                    v.tensor_copy(wr[:, :, 0:E], hi)
                    v.tensor_tensor(wr[:, :, WLO:WLO + E], weight[:], hi, ALU.subtract)
                    v.memset(wr[:, :, E:E + 1], 1.0).then_inc(w_ready, 1)
                elif kind == "stats":
                    dve.wait_ge(s_x, 16)
                    moments(x_sb, range(w * T, w * T + T))
                elif kind == "normal":
                    normal(x_sb, range(w * T, w * T + T), w + 1)
                elif kind == "weigh":
                    n, (h, e, k) = w, items[w]
                    dve.wait_ge(hid_ready, n + 1)
                    dve.wait_ge(ring_filled, ring_no[("spread", h, e)] + 1)
                    if weighed[n] == 1:
                        dve.wait_ge(values_done, LAST_UNIT)
                        dve.wait_ge(summed, B * PAIRS * (NU - 1))
                    if n >= 4:
                        dve.wait_ge(w2_done, n - 3)
                    ins = v.tensor_tensor(hid_w[:, n % 4, :], ring(ring_no[("spread", h, e)]), hid[:, n % 4, :],
                                          ALU.mult)
                    ins.then_inc(hidw_ready, 1)
                    if k == HK - 1:
                        dve.wait_ge(hidw_ready, weighed[n])
                        v.memset(freed[:], 0.0).then_inc(ring_taken, 1)
                elif kind == "out":
                    dve.wait_ge(w2_done, NI // NHALF * (w + 1))
                    v.tensor_copy(outT[:, w, :], out_bank(w)).then_inc(outT_taken, 1)
                elif kind == "back":
                    dve.wait_ge(back_filled, w + 1)
                    v.tensor_tensor(out_sb[:, w * TH:(w + 1) * TH, :],
                                    out_bank(w).rearrange("p (t d) -> p t d", t=TH),
                                    x1[:, w * TH:(w + 1) * TH, :], ALU.add).then_inc(out_ready, 1)

        @block.tensor
        def _(pe):
            mm, turn = nc.tensor.matmul, nc.tensor.transpose
            idr = ident[:]

            def three(dst, a_hi, a_lo, b_hi, b_lo, start=True, stop=True):
                mm(dst, a_hi, b_hi, start=start, stop=False)
                mm(dst, a_hi, b_lo, start=False, stop=False)
                return mm(dst, a_lo, b_hi, start=False, stop=stop)

            pe.wait_ge(consts_ready, 1)
            pe.wait_ge(s_wqk, 32)
            for c in range(PAIRS):
                ins = turn(ps[:, 0, c * D:(c + 1) * D], wq_sb[:, c * P:(c + 1) * P], idr)
            ins.then_inc(setup_filled, 1)
            for c in range(PAIRS):
                ins = turn(ps[:, 1, c * C:(c + 1) * C], wk_sb[:, c * P:(c + 1) * P], idr[0:C, 0:C])
            ins.then_inc(setup_filled, 1)
            pe.wait_ge(first_ready, 2)
            for h in range(HEADS):
                r = DH * (h % 2)
                ins = mm(ps[:, 2 + h % 2, (h // 2) * C:(h // 2 + 1) * C], wqT[r:r + DH, h // 2, :],
                         wkT[r:r + DH, h // 2, :], start=True, stop=True)
                if h >= HEADS - 2:
                    ins.then_inc(setup_filled, 1)
            pe.wait_ge(xn_ready, 1)
            for t in range(T):
                ins = turn(ps[:, 7, t * P:(t + 1) * P], xn[:, t, :], idr)
            ins.then_inc(setup_filled, 1)

            def ring_free(k):
                if k >= RING:
                    pe.wait_ge(ring_taken, k - RING + 1)

            for kind, w in steps:
                if kind == "ring":
                    k = ring_no[w]
                    dst = ring(k)
                    b = w[1]
                    ring_free(k)
                    if w[0] == "xn":
                        pe.wait_ge(xn_ready, 3 + b)
                        t0 = T + 4 * b
                        t1 = min(t0 + 4, NT)
                        for t in range(t0, t1):
                            ins = turn(dst[:, (t - t0) * P:(t - t0 + 1) * P], xn[:, t, :], idr)
                        if b == 1:
                            pe.wait_ge(s_bias, 48)
                            nb = NE * HK + 1
                            ins = turn(dst[:, (t1 - t0) * P:(t1 - t0) * P + nb], bias_rows[:, :], idr[0:nb, 0:nb])
                    elif w[0] == "turn":
                        if w[2] == 0:
                            pe.wait_ge(s_ctx[b], 32)
                        for c in range(4 * w[2], min(4 * w[2] + 4, CH)):
                            rows = P if c < FULL else REST
                            j = c - 4 * w[2]
                            ins = turn(dst[0:C, j * P:j * P + rows], ctx_raw[0:rows, b % 2, c, :],
                                       idr[0:rows, 0:rows])
                    elif w[0] == "g":
                        if b == 0 and w[2] == 0:
                            pe.wait_ge(setup_taken, 3)
                        if b and w[2] == 0:
                            pe.wait_ge(ring_taken, ring_no[("xn", 1)] + 1)
                        for i in range(2):
                            h = 2 * w[2] + i
                            q = slice(b * S, (b + 1) * S)
                            ins = three(dst[0:C, i * S:(i + 1) * S], m_hi[:, h, :], m_lo[:, h, :],
                                        xnT_hi[:, q], xnT_lo[:, q])
                    elif w[0] == "v":
                        c = w[2]
                        rows = P if c < FULL else REST
                        pe.wait_ge(w_split, 1)
                        pe.wait_ge(ring_taken, ring_no[("turn", b, c // 4)] + 1)
                        ks = slice(c * P, c * P + rows)
                        ins = three(dst[0:rows, :], ctxT_hi[0:C, b % 2, ks], ctxT_lo[:, b % 2, ks], wv_hi[:], wv_lo[:])
                    elif w[0] == "max":
                        _, b, p, i, t, blk = w
                        pe.wait_ge(ring_taken, ring_no[("g", b, p)] + 1)
                        k0 = min(blk * BW, L - BW)
                        ins = mm(dst[:, 0:BW], g_hi[0:C, b % 2, 2 * p + i, t * P:(t + 1) * P],
                                 ctxT_hi[0:C, b % 2, k0:k0 + BW], start=True, stop=True)
                    elif w[0] == "shift":
                        p = w[2]
                        pe.wait_ge(max_ready, b * PAIRS + p + 1)
                        for j in range(2 * T):
                            ins = turn(dst[0:C + 1, j * P:(j + 1) * P], neg_max[:, p % 2, j, :], idr)
                    elif w[0] == "sums":
                        pair = b * PAIRS + w[2]
                        pe.wait_ge(summed, (pair + 1) * (NU - 1))
                        for i in range(2):
                            ins = mm(dst[DH * i:DH * (i + 1), 0:S], ones[:, :],
                                     psum_keys[:, pair % 2, 0, i * S:(i + 1) * S], start=True, stop=True)
                    elif w[0] == "y":
                        pe.wait_ge(o_taken, (b + 1) * PAIRS)
                        pe.wait_ge(s_wo, 16)
                        for c in range(PAIRS):
                            ins = mm(dst[:, 0:S], wo_sb[:, c, :], oT[:, b % 2, c, :], start=(c == 0),
                                     stop=(c == PAIRS - 1))
                    elif w[0] == "yt":
                        pe.wait_ge(ring_taken, ring_no[("y", b)] + 1)
                        for t in range(T):
                            ins = turn(dst[:, t * D:(t + 1) * D], yT[:, t * P:(t + 1) * P], idr)
                    elif w[0] == "xt":
                        pe.wait_ge(xn_ready, B + b + 1)
                        for t in range(T):
                            ins = turn(dst[:, t * P:(t + 1) * P], xn[:, b * T + t, :], idr)
                    elif w[0] == "router":
                        pe.wait_ge(w_split, 3)
                        pe.wait_ge(ring_taken, ring_no[("xt", (b + 1) * B // NHALF - 1)] + 1)
                        for t in range(TH):
                            q = slice((b * TH + t) * P, (b * TH + t + 1) * P)
                            ins = three(dst[:, t * E:(t + 1) * E], xnT_hi[:, q], xnT_lo[:, q], rw_hi[:], rw_lo[:])
                    elif w[0] == "wrow":
                        pe.wait_ge(w_ready, b + 1)
                        for t in range(TH):
                            ins = turn(dst[:, t * P:(t + 1) * P], wrow[:, b * TH + t, :], idr)
                    elif w[0] == "spread":
                        h, e = w[1:]
                        pe.wait_ge(ring_taken, ring_no[("wrow", h)] + 1)
                        ins = mm(dst, select[:, e:e + 1].to_broadcast([P, P]), wT[:, h * HALF:(h + 1) * HALF],
                                 start=True, stop=True)
                    ins.then_inc(ring_filled, 1)
                elif kind == "scores":
                    b, p, u, j = w
                    n, c = unit_no(b, p, u), UNITS[u][j]
                    if n == 0 and j == 0:
                        pe.wait_ge(consts_ready, 4)
                        pe.wait_ge(v0_taken, CH)
                    if j == 0:
                        pe.wait_ge(ring_taken, ring_no[("shift", b, p)] + 1)
                        if n >= 2:
                            pe.wait_ge(probs_ready, n - 1)
                    rows = P if c < FULL else REST
                    ks = slice(c * P, c * P + rows)
                    dst = s_bank(n, j)[0:rows, :]
                    gh = g_hi[:, b % 2, 2 * p:2 * p + 2, :].rearrange("p h s -> p (h s)")
                    gl = g_lo[:, b % 2, 2 * p:2 * p + 2, :].rearrange("p h s -> p (h s)")
                    mm(dst, ctxT_hi[:, b % 2, ks], gh, start=True, stop=False)
                    mm(dst, ctxT_hi[0:C, b % 2, ks], gl, start=False, stop=False)
                    ins = mm(dst, ctxT_lo[:, b % 2, ks], gh[0:C], start=False, stop=True)
                    if c == UNITS[u][-1]:
                        ins.then_inc(scores_ready, 1)
                elif kind == "values":
                    b, p, u, j = w
                    n, pair, c = unit_no(b, p, u), b * PAIRS + p, UNITS[u][j]
                    if j == 0:
                        pe.wait_ge(probs_ready, n + 1)
                        if u == 0 and pair:
                            pe.wait_ge(o_raw_ready, pair)
                    rows = P if c < FULL else REST
                    if p == 0 and b:
                        pe.wait_ge(ring_taken, ring_no[("v", b, c)] + 1)
                    for i in range(2):
                        h = 2 * p + i
                        ins = mm(o_bank[DH * i:DH * (i + 1), :], v_sb[0:rows, c, h * DH:(h + 1) * DH],
                                 probs[0:rows, n % 4, j, i * S:(i + 1) * S], start=(c == 0), stop=(c == CH - 1))
                    if c == UNITS[u][-1]:
                        ins.then_inc(values_done, 1)
                elif kind == "v0":
                    c = w
                    rows = P if c < FULL else REST
                    pe.wait_ge(w_split, 1)
                    pe.wait_ge(ring_taken, ring_no[("turn", 0, c // 4)] + 1)
                    if c == 0:
                        pe.wait_ge(setup_taken, 2)
                    if c >= 4:
                        pe.wait_ge(v0_taken, c - 3)
                    ks = slice(c * P, c * P + rows)
                    three(ps[0:rows, c % 4, :], ctxT_hi[0:C, 0, ks], ctxT_lo[:, 0, ks], wv_hi[:], wv_lo[:]
                          ).then_inc(v0_filled, 1)
                elif kind == "first":
                    n, (h, e, k) = w, items[w]
                    if n == 0:
                        pe.wait_ge(probs_ready, LAST_UNIT)
                        pe.wait_ge(w_split, 3)
                    if n >= HB:
                        pe.wait_ge(hid_ready, n - HB + 1)
                    pe.wait_ge(ring_taken, ring_no[("xt", (h + 1) * B // NHALF - 1)] + 1)
                    q = slice(h * HALF, (h + 1) * HALF)
                    ks = slice(k * P, (k + 1) * P)
                    three(ps[:, n % HB, :], w1_hi[:, e, ks], w1_lo[:, e, ks], xnT_hi[:, q], xnT_lo[:, q]
                          ).then_inc(h_ready, 1)
                elif kind == "second":
                    n, (h, e, k) = w, items[w]
                    per = NI // NHALF
                    acc = out_bank(h)
                    if n % per == 0:
                        pe.wait_ge(o_raw_ready, B * PAIRS)
                        pe.wait_ge(s_b2, 48)
                        pe.wait_ge(s_w2, 32)
                        pe.wait_ge(ring_taken, ring_no[("wrow", h)] + 1)
                        mm(acc, b2_rows[:], wT[:, h * HALF:(h + 1) * HALF].bitcast(F32), start=True, stop=False)
                    if e == E:
                        pe.wait_ge(hid_ready, n + 1)
                        src = hid
                    else:
                        pe.wait_ge(hidw_ready, weighed[n])
                        src = hid_w
                    mm(acc, w2_sb[:, e, k, :], src[:, n % 4, :], start=False,
                       stop=(n % per == per - 1)).then_inc(w2_done, 1)
                elif kind == "back":
                    pe.wait_ge(outT_taken, w + 1)
                    for t in range(TH):
                        ins = turn(out_bank(w)[:, t * P:(t + 1) * P], outT[:, w, t * P:(t + 1) * P], idr)
                    ins.then_inc(back_filled, 1)


_INS = ["x", "ctx_768", "L0_xattn_Wq", "L0_xattn_Wk", "L0_xattn_Wv", "L0_xattn_Wo", "L0_xattn_bo",
        "L0_ffn_router_w", "L0_ffn_router_b", "L0_ffn_sw1", "L0_ffn_sb1", "L0_ffn_sw2", "L0_ffn_sb2",
        "L0_ffn_rw1", "L0_ffn_rb1", "L0_ffn_rw2", "L0_ffn_rb2"]


def kernel(**inputs):
    import numpy as _np
    import concourse.bacc as _bacc
    from concourse import mybir as _mybir
    from concourse.bass_utils import run_bass_kernel_spmd as _run

    nc = _bacc.Bacc("TRN2", target_bir_lowering=False, num_devices=1)
    arrays, args = {}, []
    for name in _INS:
        a = _np.ascontiguousarray(inputs[name])
        arrays[f"in_{name}_dram"] = a
        args.append(nc.dram_tensor(f"in_{name}_dram", a.shape, _mybir.dt.from_np(a.dtype), kind="ExternalInput").ap())
    shape = inputs["x"].shape
    out = nc.dram_tensor("out_0_dram", shape, _mybir.dt.from_np(_np.dtype("float32")), kind="ExternalOutput").ap()
    build(nc, *args, out)
    r = _run(nc, [arrays], core_ids=[0])
    return r.results[0]["out_0_dram"]
```

```python
from contextlib import ExitStack

import concourse.bass as bass
from concourse import mybir

P = 128
WARM = 22
TOP = 2
RING = 3
LAG = 2
MOST = 2
LEAD = 1.8
ALU = mybir.AluOpType
ACT = mybir.ActivationFunctionType
F32 = mybir.dt.float32
F32R = mybir.dt.float32r
AX = mybir.AxisListType
LN_EPS = 1e-5


def key_units(chunks):
    return [list(range(c, min(c + 2, chunks))) for c in range(0, chunks, 2)]


COST = {"max": 1.3, "v": 1.2, "turn": 2.4, "g": 2.4, "shift": 1.2, "y": 1.0, "yt": 6.0, "xt": 1.5, "sums": 4.5,
        "router": 2.0, "wrow": 1.0, "v0": 0.0, "stats": 2.0, "normal": 1.0,
        "xn": 2.4, "rank": 5.0}


def plan(batches, pairs, chunks, heads_per_pair, tiles, blocks, halves, experts):
    units = key_units(chunks)
    n_units = len(units)
    turns = [("turn", b, g) for b in range(batches) for g in range((chunks + 3) // 4)]
    per_batch = len(turns) // batches
    order = [(b, p) for b in range(batches) for p in range(pairs)]
    tasks = turns[:2] + [("g", 0, 0)] + turns[2:per_batch]
    n_v0 = 0
    late = []
    for n, (b, p) in enumerate(order):
        maxima = [("max", b, p, i, t, k) for i in range(heads_per_pair) for t in range(tiles)
                  for k in range(blocks)]
        put = dict(late)
        if n == 1:
            put.update({4: ("stats", 1), 8: ("stats", 2), 12: ("normal", 1)})
        if n == 2:
            put.update({3: ("stats", 3), 5: ("normal", 2), 7: ("xn", 0), 9: ("normal", 3), 11: ("xn", 1)})
        if n + 1 < len(order):
            nb, np_ = order[n + 1]
            if np_ == 0:
                for g in range(per_batch):
                    put[5 + 2 * g] = turns[nb * per_batch + g]
            put[len(maxima) - 3] = ("g", nb, np_)
        for m, task in enumerate(maxima):
            tasks.append(task)
            if n == 0 and m % 2 and n_v0 < chunks:
                tasks.append(("v0", n_v0))
                n_v0 += 1
            if m in put:
                tasks.append(put[m])
        late = [(2, ("shift", b, p))]
        if n == 0:
            rest = [("v0", c) for c in range(n_v0, chunks)]
            tasks += rest[:2] + [("shift", b, p)] + rest[2:]
            start = len(tasks)
            late = []
        if n + 1 == len(order):
            tasks.append(("shift", b, p))
    last_of = {t: n + 1 for n, t in enumerate(tasks)}
    main, held = [], []
    for b, p in order:
        q = order[order.index((b, p)) - 1] if (b, p) != (0, 0) else None
        for u, unit in enumerate(units):
            for j, c in enumerate(unit):
                if p == 0 and b:
                    main.append(("ring", ("v", b, c)))
                main.append(("scores", (b, p, u, j)))
            held += [("values", (b, p, u, j)) for j in range(len(unit))]
            if u % 2:
                main += held[:-4]
                held = held[-4:]
            elif u == n_units - 1:
                main += held[:4]
                held = held[4:]
            if q and u == 1:
                main.append(("take", q))
            if (b, p) == order[-1]:
                main += [("w2", e) for e in range(experts) if e * n_units // experts == u]
            if q and u == 2:
                main.append(("ring", ("sums",) + q))
            if q and q[1] == pairs - 1 and u in (4, 5, 6):
                main.append((("ring", ("y", q[0])), ("ring", ("yt", q[0])), ("norm", q[0]))[u - 4])
            if q and q[1] == 0 and q[0] and u == 0:
                main.append(("ring", ("xt", q[0] - 1)))
            if q and q[1] == 0 and q[0] and q[0] % (batches // halves) == 0:
                h = q[0] * halves // batches - 1
                if u in (3, 4, 6):
                    main += {3: [("ring", ("router", h)), ("exp", h)], 4: [("rank", h), ("best", h)],
                             6: [("ring", ("wrow", h))]}[u]
    main += held + [("take", order[-1])]

    def cost(x):
        return COST[x[1][0]] if x[0] == "ring" else COST.get(x[0], 0.0)

    steps = sum(kind == "scores" for kind, _ in main)
    spread = steps * (batches * pairs - LEAD) / (batches * pairs)
    total = sum(COST[t[0]] for t in tasks[start:]) + sum(cost(x) for x in main)
    def event(task):
        return (task[0], task[1]) if task[0] in ("v0", "stats", "normal") else ("ring", task)

    out, done, step, spent, last = [event(t) for t in tasks[:start]], start, 0, 0.0, None
    for x in main:
        kind, w = x
        if kind == "scores":
            step += 1
        if kind == "scores" or kind == "values" and last != "values":
            need = last_of[("shift", w[0], w[1])] if kind == "scores" else 0
            put = 0
            while done < len(tasks) and (done < need or put < MOST and spent + COST[tasks[done][0]] / 2 < total * step / spread):
                out.append(event(tasks[done]))
                spent += COST[tasks[done][0]]
                done += 1
                put += 1
        out.append(x)
        spent += cost(x)
        last = kind
    return out


def plan_experts(experts, chunks, halves, last_pair):
    b = last_pair[0]
    last = halves - 1
    amid = {2: [("ring", ("y", b))], 4: [("ring", ("xt", b))], 5: [("ring", ("router", last))]}
    behind = {0: [("ring", ("sums",) + last_pair)], 2: [("ring", ("yt", b))], 3: [("norm", b)],
              5: [("exp", last)], 6: [("rank", last)], 7: [("best", last)]}
    out, n, waiting = [], 0, []
    for h in range(halves):
        for turn, e in enumerate([experts] + list(range(experts))):
            if e < experts:
                out.append(("ring", ("spread", h, e)))
            new = list(range(n, n + chunks))
            out += [("first", i) for i in new]
            out += [("weigh", i) for i in new if e < experts]
            if h == 0:
                out += amid.get(turn, [])
            if h == 1 and turn == 0:
                out.append(("ring", ("wrow", last)))
            out += [("split", i) for i in new]
            waiting.append(new)
            if len(waiting) > LAG:
                out += [("second", i) for i in waiting.pop(0)]
            if h and turn == LAG - 1:
                out.append(("out", h - 1))
            if h and turn == LAG:
                out.append(("back", h - 1))
            if h == 0:
                out += behind.get(turn, [])
            n += chunks
    return (out + [("second", i) for new in waiting for i in new]
            + [("out", halves - 1), ("back", halves - 1)])


def build(nc, x, ctx_768, Wq, Wk, Wv, Wo, bo, router_w, router_b, sw1, sb1, sw2, sb2, rw1, rb1, rw2, rb2, out):
    B, S, D = x.shape
    L, C = ctx_768.shape[1:]
    INNER = Wq.shape[1]
    E, _, H = rw1.shape
    DH = 64
    HEADS = INNER // DH
    PAIRS = HEADS // 2
    T = S // P
    NT = B * T
    FULL = L // P
    REST = L - FULL * P
    CH = FULL + 1
    UNITS = key_units(CH)
    NU = len(UNITS)
    ROWC = C
    BLOCKS = 4
    BW = -(-L // BLOCKS)
    BW += BW % 2
    SCALE = float(DH) ** -0.5
    NE = E + 1
    HK = H // P
    HALF = 512
    NHALF = B * S // HALF
    TH = HALF // P
    WLO = 32
    assert D == P and 2 * DH == P and 0 < REST <= P and C + 1 <= P

    steps = plan(B, PAIRS, CH, 2, T, BLOCKS, NHALF, NE) + plan_experts(E, HK, NHALF, (B - 1, PAIRS - 1))
    ring_no = {w: k for k, w in enumerate(w for kind, w in steps if kind == "ring")}

    def turn_columns(g):
        return 4 * g * P, min(4 * g * P + 4 * P, L)

    def unit_no(b, p, u):
        return (b * PAIRS + p) * NU + u

    with ExitStack() as ctx:
        def sb(name, shape, dt=F32):
            return ctx.enter_context(nc.sbuf_tensor(name, shape, dt))

        def sem(name):
            return ctx.enter_context(nc.semaphore(name))

        ident = sb("ident", [P, P])
        x_sb = sb("x_sb", [P, NT, D])
        x1 = sb("x1", [P, NT, D])
        xn = sb("xn", [P, NT, D])
        stats = sb("stats", [P, NT, 6])
        mv = sb("mv", [P, NT, 2])
        veps = sb("veps", [P, NT])
        rstd = sb("rstd", [P, NT])
        neg_half = sb("neg_half", [P, NT])
        xnT_hi = sb("xnT_hi", [P, B * S], F32R)
        xnT_lo = sb("xnT_lo", [P, B * S], F32R)
        ctx_raw = sb("ctx_raw", [P, 2, CH, C])
        ctxT_hi_all = sb("ctxT_hi", [P, 2, L], F32R)
        ctxT_lo_all = sb("ctxT_lo", [P, 2, L], F32R)
        ctxT_hi, ctxT_lo = ctxT_hi_all[0:C + 1], ctxT_lo_all[0:C]
        v_sb = sb("v_sb", [P, CH, INNER])
        g_hi_all = sb("g_hi", [P, 2, HEADS, S], F32R)
        g_lo_all = sb("g_lo", [P, 2, HEADS, S], F32R)
        g_hi, g_lo = g_hi_all[0:C + 1], g_lo_all[0:C]
        early = sb("early", [P, 2, INNER])
        wq_sb = early[:, 0, :]
        wk_sb = early[0:C, 1, :]
        wv_hi = sb("wv_hi", [C, INNER], F32R)
        wv_lo = sb("wv_lo", [C, INNER], F32R)
        m_all = sb("m", [D, 2, HEADS, C], F32R)
        m_hi, m_lo = m_all[:, 0], m_all[:, 1]
        wo_sb = sb("wo_sb", [P, PAIRS, D])
        maxes = sb("maxes", [P, 2, 2 * T, BLOCKS])
        neg_max = sb("neg_max", [P, 2, 2 * T, C + 1])
        probs = sb("probs", [P, 4, 2, 2 * S])
        wv_sb = probs[0:C, 2, 0, :]
        wqT = probs[:, 3, 0, :].rearrange("p (c d) -> p c d", c=PAIRS)
        wkT = probs[:, 3, 1, 0:PAIRS * C].rearrange("p (c d) -> p c d", c=PAIRS)
        work = sb("work", [P, 2, 2 * PAIRS * S])
        psum_keys = work[:, 0, :].rearrange("p (a b c) -> p a b c", a=2, b=2)
        ones = sb("ones", [P, DH])
        rden = sb("rden", [P, S])
        o_raw = sb("o_raw", [P, S])
        oT = work[:, 1, :].rearrange("p (a b c) -> p a b c", a=2, b=PAIRS)
        yT = sb("yT", [P, S])
        freed = sb("freed", [1, 1])
        bias_rows = sb("bias_rows", [NE * HK + 1, P])
        biasT = sb("biasT", [P, NE * HK + 1])
        w1_sb = work[:].rearrange("p a b -> p (a b)")[:, 0:NE * H].rearrange("p (e h) -> p e h", e=NE)
        w1_hi = sb("w1_hi", [D, NE, H], F32R)
        w1_lo = sb("w1_lo", [D, NE, H], F32R)
        w2_hi = sb("w2_hi", [P, NE, HK, D], F32R)
        w2_sb = ctx_raw[:].rearrange("p a b c -> p (a b c)")[:, 0:NE * HK * D].rearrange(
            "p (e k d) -> p e k d", e=NE, k=HK)
        rw_sb = sb("rw_sb", [D, E])
        rw_hi = sb("rw_hi", [D, E], F32R)
        rw_lo = sb("rw_lo", [D, E], F32R)
        rb_sb = sb("rb_sb", [P, E])
        b2_rows = sb("b2_rows", [P, D])
        select = sb("select", [P, E], F32R)
        selectf = sb("selectf", [P, E])
        before = sb("before", [P, E, E])
        logit = sb("logit", [P, TH, E])
        lmax = sb("lmax", [P, TH])
        lexp = sb("lexp", [P, TH, E])
        lsum = sb("lsum", [P, TH])
        rsum = sb("rsum", [P, TH])
        rprob = sb("rprob", [P, TH, E])
        beats = sb("beats", [P, TH, E, E])
        ties = sb("ties", [P, TH, E, E])
        rank = sb("rank", [P, TH, E])
        weight = sb("weight", [P, TH, E])
        wrow = early[:].rearrange("p a b -> p (a b)").rearrange("p (t r) -> p t r", t=NT)
        wT = sb("wT", [P, B * S], F32R)
        w_hi = sb("w_hi", [P, TH, E], F32R)
        outT = xn[:].rearrange("p (h t) d -> p h (t d)", h=NHALF)
        out_sb = x_sb
        hid = probs[:, 0:2, :, :].rearrange("p a b c -> p (a b) c")
        hid_w = probs[:, 2:4, :, :].rearrange("p a b c -> p (a b) c")

        hid_hi, hid_lo = (t[:].rearrange("p a h s -> p (a h s)").rearrange("p (n c) -> p n c", c=HALF)
                          for t in (g_hi_all, g_lo_all))
        SPLITS = hid_hi.shape[1]

        def w2_lo(e):
            per = L // (HK * D)
            t = (ctxT_hi_all, ctxT_lo_all)[e // per]
            return t[:, B % 2, e % per * HK * D:(e % per + 1) * HK * D].rearrange("p (k d) -> p k d", k=HK)

        ps = ctx.enter_context(nc.psum_tensor("ps", [P, 8, 512], F32))

        def s_bank(n, c):
            return ps[:, 2 * (n % 2) + c, :]

        def ring(k):
            return ps[:, 4 + k % RING, :]

        o_bank = ps[:, 4 + RING, 0:S]
        HB = 3

        def out_bank(h):
            return ps[:, (7, 3)[h % 2], :]

        s_wqk, s_x0, s_x, s_wv = sem("loaded_wqk"), sem("loaded_x0"), sem("loaded_x"), sem("loaded_wv")
        s_ctx = [sem(f"loaded_ctx{b}") for b in range(B)]
        s_wo, s_bias, s_w1, s_w2 = sem("loaded_wo"), sem("loaded_bias"), sem("loaded_w1"), sem("loaded_w2")
        s_rw, s_b2 = sem("loaded_router"), sem("loaded_b2")
        pool_done = sem("pool_done")
        consts_ready = sem("consts_ready")
        w_split = sem("w_split")
        rstd_ready = sem("rstd_ready")
        var_ready = sem("var_ready")
        dve_done = sem("dve_done")
        setup_filled = sem("setup_filled")
        setup_taken = sem("setup_taken")
        xn_ready = sem("xn_ready")
        s_bias_turned = sem("bias_turned")
        ring_filled = sem("ring_filled")
        ring_taken = sem("ring_taken")
        max_ready = sem("max_ready")
        scores_ready = sem("scores_ready")
        probs_ready = sem("probs_ready")
        values_done = sem("values_done")
        summed = sem("summed")
        sums_ready = sem("sums_ready")
        o_raw_ready = sem("o_raw_ready")
        o_taken = sem("o_taken")
        v0_filled, v0_taken = sem("v0_filled"), sem("v0_taken")
        first_ready = sem("first_ready")
        turn_hi = sem("turn_hi")
        logit_ready, lexp_ready, w_ready = sem("logit_ready"), sem("lexp_ready"), sem("w_ready")
        h_ready, hid_ready, hidw_ready = sem("h_ready"), sem("hid_ready"), sem("hidw_ready")
        hid_hi_ready, hid_lo_ready = sem("hid_hi_ready"), sem("hid_lo_ready")
        w2_split = sem("w2_split")
        w2_done = sem("w2_done")
        outT_taken = sem("outT_taken")
        back_filled, out_ready, s_out = sem("back_filled"), sem("out_ready"), sem("stored")

        def activations(n):
            return (hid if items[n][1] == E else hid_w)[:, n % 4, :]

        def m_parts(i):
            hp = PAIRS // 2
            hi, lo = (m.rearrange("p (a two) c -> p two a c", two=2)[:, :, i * hp:(i + 1) * hp, :]
                      for m in (m_hi, m_lo))
            return hi, lo, ps[:, (2, 0)[i]:(4, 2)[i], 0:hp * C].rearrange("p two (a c) -> p two a c", a=hp)

        block = ctx.enter_context(nc.Block())
        items = [(h, e, k) for h in range(NHALF) for e in [E] + list(range(E)) for k in range(HK)]
        NI = len(items)
        LAST_LO = NI - HK
        weighed, count = {}, 0
        for n, (h, e, k) in enumerate(items):
            count += e < E
            weighed[n] = count
        LAST_UNIT = B * PAIRS * NU
        LAST_PAIR = (B - 1, PAIRS - 1)
        assert (LAST_UNIT - 1) % 4 == 3

        def add_probabilities(ops, engine, then_own, w):
            b, p, u, _ = w
            n, pair = unit_no(b, p, u), b * PAIRS + p
            acc = psum_keys[:, pair % 2]
            if u == 0:
                return
            engine.wait_ge(summed, pair * (NU - 1) + u - 1)
            engine.wait_ge(probs_ready, n + 1)
            pr = probs[:, n % 4]
            if u == 1:
                if pair >= 2:
                    engine.wait_ge(ring_filled, ring_no[("sums",) + divmod(pair - 2, PAIRS)] + 1)
                ops.tensor_tensor(acc, probs[:, (n - 1) % 4], pr, ALU.add).then_inc(summed, 1)
            elif u < NU - 1:
                ops.tensor_tensor(acc, acc, pr, ALU.add).then_inc(summed, 1)
            else:
                then_own(ops.tensor_tensor(acc[:, 0], acc[:, 0], acc[:, 1], ALU.add))
                ops.tensor_tensor(acc[0:REST, 0], acc[0:REST, 0], pr[0:REST, 0], ALU.add).then_inc(summed, 1)

        @block.sync
        def _(sp):
            sp.dma_start(wq_sb[:], Wq).then_inc(s_wqk, 16)
            sp.dma_start(wk_sb[:], Wk).then_inc(s_wqk, 16)
            for b in range(B):
                if b >= 2:
                    sp.wait_ge(ring_taken, ring_no[("turn", b - 2, (CH + 3) // 4 - 1)] + 1)
                sp.dma_start(ctx_raw[:, b % 2, 0:FULL, :],
                             ctx_768[b, 0:FULL * P].rearrange("(p j) d -> p j d", j=FULL)).then_inc(s_ctx[b], 16)
                sp.dma_start(ctx_raw[0:REST, b % 2, FULL, :], ctx_768[b, FULL * P:L]).then_inc(s_ctx[b], 16)
                if b == 0:
                    sp.dma_start(wv_sb, Wv).then_inc(s_wv, 16)
                    sp.dma_start(w1_sb[:, 0:E], rw1.rearrange("e d h -> d e h")).then_inc(s_w1, 16)
                    sp.dma_start(w1_sb[:, E], sw1).then_inc(s_w1, 16)
                    sp.dma_start(rw_sb[:], router_w).then_inc(s_rw, 16)
                    sp.dma_start(rb_sb[:], router_b.rearrange("(o e) -> o e", o=1).to_broadcast([P, E])
                                 ).then_inc(s_rw, 16)
                    sp.dma_start(bias_rows[0:E * HK], rb1.rearrange("e (k p) -> (e k) p", p=P)).then_inc(s_bias, 16)
                    sp.dma_start(bias_rows[E * HK:NE * HK], sb1.rearrange("(k p) -> k p", p=P)).then_inc(s_bias, 16)
                    sp.dma_start(bias_rows[NE * HK:NE * HK + 1], bo.rearrange("(k p) -> k p", p=P)
                                 ).then_inc(s_bias, 16)
                if b == 1:
                    sp.dma_start(wo_sb[:], Wo.rearrange("(c p) d -> p c d", p=P)).then_inc(s_wo, 16)
                    sp.wait_ge(pool_done, 4)
                    sp.dma_start(b2_rows[0:E], rb2).then_inc(s_b2, 16)
                    sp.dma_start(b2_rows[WLO:WLO + E], rb2).then_inc(s_b2, 16)
                    sp.dma_start(b2_rows[E:E + 1], sb2.rearrange("(o d) -> o d", o=1)).then_inc(s_b2, 16)
            sp.wait_ge(ring_taken, ring_no[("turn", B - 1, (CH + 3) // 4 - 1)] + 1)
            sp.dma_start(w2_sb[:, 0:E], rw2.rearrange("e (k p) d -> p e k d", p=P)).then_inc(s_w2, 16)
            sp.dma_start(w2_sb[:, E], sw2.rearrange("(k p) d -> p k d", p=P)).then_inc(s_w2, 16)
            for h in range(NHALF):
                sp.wait_ge(out_ready, h + 1)
                bb = HALF // S
                sp.dma_start(out[h * bb:(h + 1) * bb].rearrange("b (p j) d -> p b (j d)", j=T),
                             out_sb[:, h * TH:(h + 1) * TH, :].rearrange("p (b j) d -> p b (j d)", j=T)
                             ).then_inc(s_out, 16)
            sp.wait_ge(s_out, 16 * NHALF)

        @block.gpsimd
        def _(pool):
            g = nc.gpsimd
            done = [0]

            def own(ins):
                done[0] += 1
                ins.then_inc(pool_done, 1)

            def then_own(ins):
                own(ins)
                pool.wait_ge(pool_done, done[0])

            def inverse_roots(tiles, round_no):
                pool.wait_ge(var_ready, round_no)
                g.tensor_tensor(rstd[:, tiles], veps[:, tiles], neg_half[:, tiles], ALU.pow).then_inc(rstd_ready, 1)

            own(g.memset(ones[:], 1.0))
            own(g.memset(neg_half[:], -0.5))
            then_own(g.memset(ident[:], 0.0))
            g.affine_select(out=ident[:], in_=ident[:], compare_op=ALU.not_equal, fill=1.0, base=0,
                            pattern=[[-1, P]], channel_multiplier=1).then_inc(consts_ready, 1)
            for ap, value in ((b2_rows, 0.0), (neg_max, 0.0), (selectf, 0.0)):
                own(g.memset(ap[:], value))
            then_own(g.memset(before[:], 1.0))
            inverse_roots(slice(0, T), 1)
            pool.wait_ge(s_wv, 16)
            then_own(g.tensor_copy(wv_hi[:], wv_sb))
            g.tensor_tensor(wv_lo[:], wv_sb, wv_hi[:].bitcast(F32), ALU.subtract).then_inc(w_split, 1)
            for base in (0, -WLO):
                then_own(g.affine_select(out=selectf[:], in_=selectf[:], compare_op=ALU.not_equal, fill=1.0,
                                         base=base, pattern=[[-1, E]], channel_multiplier=1))
            g.tensor_copy(select[:], selectf[:]).then_inc(consts_ready, 1)
            g.affine_select(out=before[:], in_=before[:], compare_op=ALU.is_gt, fill=0.0, base=0,
                            pattern=[[1, E], [-1, E]], channel_multiplier=0).then_inc(consts_ready, 1)
            pool.wait_ge(consts_ready, 3)
            g.memset(ctxT_hi[C:C + 1, :, :].bitcast(F32), 1.0).then_inc(consts_ready, 1)
            pool.wait_ge(consts_ready, 4)
            pool.wait_ge(s_w1, 32)
            pool.wait_ge(s_rw, 32)
            own(g.tensor_copy(w1_hi[:], w1_sb))
            then_own(g.tensor_copy(rw_hi[:], rw_sb[:]))
            g.tensor_tensor(w1_lo[:], w1_sb, w1_hi[:].bitcast(F32), ALU.subtract).then_inc(w_split, 1)
            g.tensor_tensor(rw_lo[:], rw_sb[:], rw_hi[:].bitcast(F32), ALU.subtract).then_inc(w_split, 1)

            pool.wait_ge(w_split, 3)
            for kind, w in steps:
                if kind == "stats":
                    inverse_roots(slice(w * T, w * T + T), w + 1)
                if kind == "ring" and w[0] == "yt":
                    inverse_roots(slice(w[1] * T, w[1] * T + T), B + w[1] + 1)
                if kind == "split":
                    if w >= LAST_LO:
                        continue
                    pool.wait_ge(hid_hi_ready, w + 1)
                    if w >= SPLITS:
                        pool.wait_ge(w2_done, w - SPLITS + 1)
                    g.tensor_tensor(hid_lo[:, w % SPLITS, :], activations(w), hid_hi[:, w % SPLITS, :].bitcast(F32),
                                    ALU.subtract).then_inc(hid_lo_ready, 1)
                if kind != "scores" or w[3]:
                    continue
                if w[:2] != LAST_PAIR:
                    add_probabilities(g, pool, then_own, w)

        @block.scalar
        def _(act):
            xv = x_sb[:].rearrange("p (b j) d -> p b (j d)", j=T)
            xd = x.rearrange("b (p j) d -> p b (j d)", j=T)
            act.dma_start(xv[:, 0:1], xd[:, 0:1]).then_inc(s_x0, 16)
            act.dma_start(xv[:, 1:B], xd[:, 1:B]).then_inc(s_x, 16)
            act.wait_ge(setup_filled, 1)
            nc.scalar.copy(wqT, ps[:, 0, :].rearrange("p (c d) -> p c d", c=PAIRS)).then_inc(first_ready, 1)
            act.wait_ge(setup_filled, 2)
            nc.scalar.copy(wkT, ps[:, 1, 0:PAIRS * C].rearrange("p (c d) -> p c d", c=PAIRS)
                           ).then_inc(first_ready, 1)
            act.wait_ge(setup_filled, 4)
            hi, _, src = m_parts(1)
            nc.scalar.copy(hi, src).then_inc(first_ready, 1)
            for kind, w in steps:
                if kind == "ring" and w[0] == "turn" and w[1] == 0:
                    act.wait_ge(ring_filled, ring_no[w] + 1)
                    c0, c1 = turn_columns(w[2])
                    nc.scalar.copy(ctxT_hi[0:C, 0, c0:c1], ring(ring_no[w])[0:C, 0:c1 - c0]).then_inc(turn_hi, 1)
                elif kind == "v0":
                    rows = P if w < FULL else REST
                    act.wait_ge(v0_filled, w + 1)
                    nc.scalar.copy(v_sb[0:rows, w, :], ps[0:rows, w % 4, :]).then_inc(v0_taken, 1)
                elif kind == "scores" and w[3] == 0:
                    n, u = unit_no(*w[:3]), w[2]
                    act.wait_ge(scores_ready, n + 1)
                    if n == 2:
                        act.wait_ge(w_split, 1)
                    if n >= 4:
                        act.wait_ge(values_done, n - 3)
                        pair, uu = (n - 4) // NU, (n - 4) % NU
                        act.wait_ge(summed, pair * (NU - 1) + max(uu, 1))
                    wide = len(UNITS[u])
                    rows = P if wide == 2 else REST
                    s = ps[0:rows, 2 * (n % 2):2 * (n % 2) + wide, :]
                    nc.scalar.activation(probs[0:rows, n % 4, 0:wide, :], s, ACT.Exp,
                                         scale=SCALE).then_inc(probs_ready, 1)
                elif kind == "take":
                    pair = w[0] * PAIRS + w[1]
                    act.wait_ge(values_done, NU * (pair + 1))
                    if pair:
                        act.wait_ge(o_taken, pair)
                    nc.scalar.copy(o_raw[:], o_bank).then_inc(o_raw_ready, 1)
                elif kind == "exp":
                    act.wait_ge(logit_ready, w + 1)
                    nc.scalar.activation(lexp[:], logit[:], ACT.Exp).then_inc(lexp_ready, 1)
                elif kind == "first":
                    n, e, k = w, items[w][1], items[w][2]
                    act.wait_ge(h_ready, n + 1)
                    if n == 0:
                        act.wait_ge(s_bias_turned, 1)
                        act.wait_ge(values_done, LAST_UNIT - 1)
                        act.wait_ge(summed, B * PAIRS * (NU - 1) - 2)
                    if n >= 4:
                        if items[n - 4][1] == E:
                            act.wait_ge(hid_lo_ready, n - 3)
                        else:
                            act.wait_ge(hidw_ready, weighed[n - 4])
                    c = e * HK + k
                    nc.scalar.activation(hid[:, n % 4, :], ps[:, n % HB, :], ACT.Gelu,
                                         bias=biasT[:, c:c + 1]).then_inc(hid_ready, 1)

        @block.vector
        def _(dve):
            v = nc.vector
            count = [0]

            def then_own(ins):
                count[0] += 1
                ins.then_inc(dve_done, 1)
                dve.wait_ge(dve_done, count[0])

            def halves(hi, lo, src, signal):
                then_own(v.tensor_copy(hi, src))
                v.tensor_tensor(lo, src, hi.bitcast(F32), ALU.subtract).then_inc(signal, 1)

            def moments(src, tiles):
                for t in tiles:
                    ins = v.bn_stats(stats[:, t, :], src[:, t, :])
                then_own(ins)
                for t in tiles:
                    ins = v.bn_aggr(mv[:, t, :], stats[:, t, :])
                then_own(ins)
                ts = slice(tiles[0], tiles[-1] + 1)
                v.tensor_scalar(veps[:, ts], mv[:, ts, 1], LN_EPS, None, ALU.add).then_inc(var_ready, 1)

            def normal(src, tiles, round_no):
                dve.wait_ge(rstd_ready, round_no)
                for t in tiles:
                    ins = v.tensor_scalar(xn[:, t, :], src[:, t, :], mv[:, t, 0:1], rstd[:, t:t + 1],
                                          ALU.subtract, ALU.mult)
                ins.then_inc(xn_ready, 1)

            dve.wait_ge(s_x0, 16)
            moments(x_sb, range(T))
            normal(x_sb, range(T), 1)
            dve.wait_ge(setup_filled, 3)
            halves(*m_parts(0), setup_taken)
            dve.wait_ge(setup_filled, 5)
            halves(xnT_hi[:, 0:S], xnT_lo[:, 0:S], ps[:, 7, 0:S], setup_taken)
            dve.wait_ge(first_ready, 3)
            hi, lo, src = m_parts(1)
            v.tensor_tensor(lo, src, hi.bitcast(F32), ALU.subtract).then_inc(setup_taken, 1)

            for kind, w in steps:
                if kind == "scores" and w[:2] == LAST_PAIR and w[3] == 0:
                    add_probabilities(v, dve, then_own, w)
                if kind == "ring":
                    k = ring_no[w]
                    src = ring(k)
                    dve.wait_ge(ring_filled, k + 1)
                    b = w[1]
                    if w[0] == "xn":
                        t0 = T + 4 * b
                        t1 = min(t0 + 4, NT)
                        if b == 1:
                            v.tensor_copy(biasT[:], src[:, P * (t1 - t0):P * (t1 - t0) + NE * HK + 1]
                                          ).then_inc(s_bias_turned, 1)
                        halves(xnT_hi[:, t0 * P:t1 * P], xnT_lo[:, t0 * P:t1 * P], src[:, 0:(t1 - t0) * P], ring_taken)
                    elif w[0] == "turn":
                        c0, c1 = turn_columns(w[2])
                        if w[2] == 0 and b >= 2:
                            dve.wait_ge(scores_ready, unit_no(b - 2, PAIRS - 1, NU - 1) + 1)
                        if b == 0:
                            dve.wait_ge(turn_hi, w[2] + 1)
                            v.tensor_tensor(ctxT_lo[:, 0, c0:c1], src[0:C, 0:c1 - c0],
                                            ctxT_hi[0:C, 0, c0:c1].bitcast(F32), ALU.subtract
                                            ).then_inc(ring_taken, 1)
                            continue
                        halves(ctxT_hi[0:C, b % 2, c0:c1], ctxT_lo[:, b % 2, c0:c1], src[0:C, 0:c1 - c0], ring_taken)
                    elif w[0] == "g":
                        hs = slice(2 * w[2], 2 * w[2] + 2)
                        gv = src[0:C, :].rearrange("p (h s) -> p h s", h=2)
                        halves(g_hi[0:C, b % 2, hs, :], g_lo[:, b % 2, hs, :], gv, ring_taken)
                    elif w[0] == "v":
                        c = w[2]
                        rows = P if c < FULL else REST
                        if b >= 1:
                            dve.wait_ge(values_done, unit_no(b - 1, PAIRS - 1, c // 2) + 1)
                        v.tensor_copy(v_sb[0:rows, c, :], src[0:rows, :]).then_inc(ring_taken, 1)
                    elif w[0] == "max":
                        _, b, p, i, t, blk = w
                        v.tensor_reduce(maxes[:, p % 2, i * T + t, blk:blk + 1], src[:, 0:BW], AX.X,
                                        ALU.max).then_inc(ring_taken, 1)
                        if (i, t, blk) == (1, T - 1, BLOCKS - 1):
                            dve.wait_ge(ring_taken, k + 1)
                            v.tensor_reduce(neg_max[:, p % 2, :, C], maxes[:, p % 2, :, :], AX.X, ALU.max,
                                            negate=True).then_inc(max_ready, 1)
                    elif w[0] == "shift":
                        p = w[2]
                        v.tensor_copy(g_hi[C:C + 1, b % 2, 2 * p:2 * p + 2, :],
                                      src[C:C + 1, :].rearrange("p (h s) -> p h s", h=2)).then_inc(ring_taken, 1)
                    elif w[0] == "sums":
                        pair = b * PAIRS + w[2]
                        if pair:
                            dve.wait_ge(o_taken, pair)
                        v.reciprocal(rden[:], src[:, 0:S]).then_inc(ring_taken, 1)
                        dve.wait_ge(ring_taken, k + 1)
                        dve.wait_ge(o_raw_ready, pair + 1)
                        v.tensor_tensor(oT[:, b % 2, w[2], :], o_raw[:], rden[:], ALU.mult).then_inc(o_taken, 1)
                    elif w[0] == "y":
                        v.tensor_scalar(yT[:], src[:, 0:S], biasT[:, NE * HK:NE * HK + 1], None,
                                        ALU.add).then_inc(ring_taken, 1)
                    elif w[0] == "yt":
                        tiles = range(b * T, (b + 1) * T)
                        v.tensor_tensor(x1[:, b * T:(b + 1) * T, :], src[:, 0:T * D].rearrange("p (t d) -> p t d", t=T),
                                        x_sb[:, b * T:(b + 1) * T, :], ALU.add).then_inc(ring_taken, 1)
                        dve.wait_ge(ring_taken, k + 1)
                        moments(x1, tiles)
                    elif w[0] == "xt":
                        halves(xnT_hi[:, b * S:(b + 1) * S], xnT_lo[:, b * S:(b + 1) * S], src[:, 0:S], ring_taken)
                    elif w[0] == "router":
                        if b == 0:
                            dve.wait_ge(s_rw, 32)
                            then_own(v.memset(wrow, 0.0))
                        then_own(v.tensor_tensor(logit[:], src[:, 0:TH * E].rearrange("p (t e) -> p t e", e=E),
                                                 rb_sb[:].unsqueeze(1).to_broadcast([P, TH, E]), ALU.add))
                        then_own(v.tensor_reduce(lmax[:], logit[:], AX.X, ALU.max))
                        v.tensor_tensor(logit[:], logit[:], lmax[:].unsqueeze(2).to_broadcast([P, TH, E]),
                                        ALU.subtract).then_inc(logit_ready, 1)
                        dve.wait_ge(logit_ready, b + 1)
                        v.memset(freed[:], 0.0).then_inc(ring_taken, 1)
                    elif w[0] == "wrow":
                        v.tensor_copy(wT[:, b * HALF:(b + 1) * HALF], src).then_inc(ring_taken, 1)
                elif kind == "norm":
                    normal(x1, range(w * T, (w + 1) * T), B + w + 1)
                elif kind == "rank":
                    dve.wait_ge(lexp_ready, w + 1)
                    then_own(v.tensor_reduce(lsum[:], lexp[:], AX.X, ALU.add))
                    then_own(v.reciprocal(rsum[:], lsum[:]))
                    then_own(v.tensor_tensor(rprob[:], lexp[:], rsum[:].unsqueeze(2).to_broadcast([P, TH, E]),
                                             ALU.mult))
                    dve.wait_ge(consts_ready, 3)
                    for t in range(TH):
                        of_j = rprob[:, t, :].unsqueeze(1).to_broadcast([P, E, E])
                        of_e = rprob[:, t, :].unsqueeze(2).to_broadcast([P, E, E])
                        v.tensor_tensor(beats[:, t], of_j, of_e, ALU.is_gt)
                        ins = v.tensor_tensor(ties[:, t], of_j, of_e, ALU.is_equal)
                    then_own(ins)
                elif kind == "best":
                    then_own(v.tensor_tensor(ties[:], ties[:], before[:].unsqueeze(1).to_broadcast([P, TH, E, E]),
                                             ALU.mult))
                    then_own(v.tensor_tensor(beats[:], beats[:], ties[:], ALU.add))
                    then_own(v.tensor_reduce(rank[:], beats[:], AX.X, ALU.add))
                    then_own(v.scalar_tensor_tensor(weight[:], rank[:], float(TOP), rprob[:], ALU.is_lt, ALU.mult))
                    then_own(v.tensor_copy(w_hi[:], weight[:]))
                    hi = w_hi[:].bitcast(F32)
                    wr = wrow[:, w * TH:(w + 1) * TH, :]
                    v.tensor_copy(wr[:, :, 0:E], hi)
                    v.tensor_tensor(wr[:, :, WLO:WLO + E], weight[:], hi, ALU.subtract)
                    v.memset(wr[:, :, E:E + 1], 1.0).then_inc(w_ready, 1)
                elif kind == "stats":
                    dve.wait_ge(s_x, 16)
                    moments(x_sb, range(w * T, w * T + T))
                elif kind == "normal":
                    normal(x_sb, range(w * T, w * T + T), w + 1)
                elif kind == "weigh":
                    n, (h, e, k) = w, items[w]
                    dve.wait_ge(hid_ready, n + 1)
                    dve.wait_ge(ring_filled, ring_no[("spread", h, e)] + 1)
                    if weighed[n] == 1:
                        dve.wait_ge(values_done, LAST_UNIT)
                        dve.wait_ge(summed, B * PAIRS * (NU - 1))
                    if n >= 4:
                        dve.wait_ge(hid_lo_ready, n - 3)
                    ins = v.tensor_tensor(hid_w[:, n % 4, :], ring(ring_no[("spread", h, e)]), hid[:, n % 4, :],
                                          ALU.mult)
                    ins.then_inc(hidw_ready, 1)
                    if k == HK - 1:
                        dve.wait_ge(hidw_ready, weighed[n])
                        v.memset(freed[:], 0.0).then_inc(ring_taken, 1)
                elif kind == "split":
                    n, e = w, items[w][1]
                    if n == 0:
                        dve.wait_ge(scores_ready, LAST_UNIT)
                    if n >= SPLITS:
                        dve.wait_ge(w2_done, n - SPLITS + 1)
                    if e == E:
                        dve.wait_ge(hid_ready, n + 1)
                    else:
                        dve.wait_ge(hidw_ready, weighed[n])
                    v.tensor_copy(hid_hi[:, n % SPLITS, :], activations(n)).then_inc(hid_hi_ready, 1)
                    if n >= LAST_LO:
                        dve.wait_ge(hid_hi_ready, n + 1)
                        if n == LAST_LO:
                            dve.wait_ge(hid_lo_ready, n)
                        v.tensor_tensor(hid_lo[:, n % SPLITS, :], activations(n),
                                        hid_hi[:, n % SPLITS, :].bitcast(F32), ALU.subtract
                                        ).then_inc(hid_lo_ready, 1)
                elif kind == "w2":
                    if w == 0:
                        dve.wait_ge(s_w2, 32)
                        dve.wait_ge(scores_ready, unit_no(B - 1, 0, 0))
                    halves(w2_hi[:, w], w2_lo(w), w2_sb[:, w], w2_split)
                elif kind == "out":
                    dve.wait_ge(w2_done, NI // NHALF * (w + 1))
                    v.tensor_copy(outT[:, w, :], out_bank(w)).then_inc(outT_taken, 1)
                elif kind == "back":
                    dve.wait_ge(back_filled, w + 1)
                    v.tensor_tensor(out_sb[:, w * TH:(w + 1) * TH, :],
                                    out_bank(w).rearrange("p (t d) -> p t d", t=TH),
                                    x1[:, w * TH:(w + 1) * TH, :], ALU.add).then_inc(out_ready, 1)

        @block.tensor
        def _(pe):
            mm, turn = nc.tensor.matmul, nc.tensor.transpose
            idr = ident[:]

            def three(dst, a_hi, a_lo, b_hi, b_lo, start=True, stop=True):
                mm(dst, a_hi, b_hi, start=start, stop=False)
                mm(dst, a_hi, b_lo, start=False, stop=False)
                return mm(dst, a_lo, b_hi, start=False, stop=stop)

            pe.wait_ge(pool_done, 1)
            for _ in range(WARM):
                mm(ps[0:DH, 4, 0:DH], ones[:], ones[:], start=True, stop=True)
            pe.wait_ge(consts_ready, 1)
            pe.wait_ge(s_wqk, 32)
            for c in range(PAIRS):
                ins = turn(ps[:, 0, c * D:(c + 1) * D], wq_sb[:, c * P:(c + 1) * P], idr)
            ins.then_inc(setup_filled, 1)
            for c in range(PAIRS):
                ins = turn(ps[:, 1, c * C:(c + 1) * C], wk_sb[:, c * P:(c + 1) * P], idr[0:C, 0:C])
            ins.then_inc(setup_filled, 1)
            pe.wait_ge(first_ready, 2)
            for h in range(HEADS):
                r = DH * (h % 2)
                i, j = divmod(h, HEADS // 2)
                ins = mm(ps[:, (2, 0)[i] + h % 2, (j // 2) * C:(j // 2 + 1) * C], wqT[r:r + DH, h // 2, :],
                         wkT[r:r + DH, h // 2, :], start=True, stop=True)
                if h % (HEADS // 2) == HEADS // 2 - 1:
                    ins.then_inc(setup_filled, 1)
            pe.wait_ge(xn_ready, 1)
            for t in range(T):
                ins = turn(ps[:, 7, t * P:(t + 1) * P], xn[:, t, :], idr)
            ins.then_inc(setup_filled, 1)

            def ring_free(k):
                if k >= RING:
                    pe.wait_ge(ring_taken, k - RING + 1)

            for kind, w in steps:
                if kind == "ring":
                    k = ring_no[w]
                    dst = ring(k)
                    b = w[1]
                    ring_free(k)
                    if w[0] == "xn":
                        pe.wait_ge(xn_ready, 3 + b)
                        t0 = T + 4 * b
                        t1 = min(t0 + 4, NT)
                        for t in range(t0, t1):
                            ins = turn(dst[:, (t - t0) * P:(t - t0 + 1) * P], xn[:, t, :], idr)
                        if b == 1:
                            pe.wait_ge(s_bias, 48)
                            nb = NE * HK + 1
                            ins = turn(dst[:, (t1 - t0) * P:(t1 - t0) * P + nb], bias_rows[:, :], idr[0:nb, 0:nb])
                    elif w[0] == "turn":
                        if w[2] == 0:
                            pe.wait_ge(s_ctx[b], 32)
                        for c in range(4 * w[2], min(4 * w[2] + 4, CH)):
                            rows = P if c < FULL else REST
                            j = c - 4 * w[2]
                            ins = turn(dst[0:C, j * P:j * P + rows], ctx_raw[0:rows, b % 2, c, :],
                                       idr[0:rows, 0:rows])
                    elif w[0] == "g":
                        if b == 0:
                            pe.wait_ge(setup_taken, 2 if w[2] < PAIRS // 2 else 3)
                        if b and w[2] == 0:
                            pe.wait_ge(ring_taken, ring_no[("xn", 1)] + 1)
                        for i in range(2):
                            h = 2 * w[2] + i
                            q = slice(b * S, (b + 1) * S)
                            ins = three(dst[0:C, i * S:(i + 1) * S], m_hi[:, h, :], m_lo[:, h, :],
                                        xnT_hi[:, q], xnT_lo[:, q])
                    elif w[0] == "v":
                        c = w[2]
                        rows = P if c < FULL else REST
                        pe.wait_ge(w_split, 1)
                        pe.wait_ge(ring_taken, ring_no[("turn", b, c // 4)] + 1)
                        ks = slice(c * P, c * P + rows)
                        ins = three(dst[0:rows, :], ctxT_hi[0:C, b % 2, ks], ctxT_lo[:, b % 2, ks], wv_hi[:], wv_lo[:])
                    elif w[0] == "max":
                        _, b, p, i, t, blk = w
                        k0 = min(blk * BW, L - BW)
                        pe.wait_ge(ring_taken, max(ring_no[("g", b, p)],
                                                   ring_no[("turn", b, (k0 + BW - 1) // (4 * P))]) + 1)
                        ins = mm(dst[:, 0:BW], g_hi[0:C, b % 2, 2 * p + i, t * P:(t + 1) * P],
                                 ctxT_hi[0:C, b % 2, k0:k0 + BW], start=True, stop=True)
                    elif w[0] == "shift":
                        p = w[2]
                        pe.wait_ge(max_ready, b * PAIRS + p + 1)
                        for j in range(2 * T):
                            ins = turn(dst[0:C + 1, j * P:(j + 1) * P], neg_max[:, p % 2, j, :], idr)
                    elif w[0] == "sums":
                        pair = b * PAIRS + w[2]
                        pe.wait_ge(summed, (pair + 1) * (NU - 1))
                        for i in range(2):
                            ins = mm(dst[DH * i:DH * (i + 1), 0:S], ones[:, :],
                                     psum_keys[:, pair % 2, 0, i * S:(i + 1) * S], start=True, stop=True)
                    elif w[0] == "y":
                        pe.wait_ge(o_taken, (b + 1) * PAIRS)
                        pe.wait_ge(s_wo, 16)
                        for c in range(PAIRS):
                            ins = mm(dst[:, 0:S], wo_sb[:, c, :], oT[:, b % 2, c, :], start=(c == 0),
                                     stop=(c == PAIRS - 1))
                    elif w[0] == "yt":
                        pe.wait_ge(ring_taken, ring_no[("y", b)] + 1)
                        for t in range(T):
                            ins = turn(dst[:, t * D:(t + 1) * D], yT[:, t * P:(t + 1) * P], idr)
                    elif w[0] == "xt":
                        pe.wait_ge(xn_ready, B + b + 1)
                        for t in range(T):
                            ins = turn(dst[:, t * P:(t + 1) * P], xn[:, b * T + t, :], idr)
                    elif w[0] == "router":
                        pe.wait_ge(w_split, 3)
                        pe.wait_ge(ring_taken, ring_no[("xt", (b + 1) * B // NHALF - 1)] + 1)
                        for t in range(TH):
                            q = slice((b * TH + t) * P, (b * TH + t + 1) * P)
                            ins = three(dst[:, t * E:(t + 1) * E], xnT_hi[:, q], xnT_lo[:, q], rw_hi[:], rw_lo[:])
                    elif w[0] == "wrow":
                        pe.wait_ge(w_ready, b + 1)
                        for t in range(TH):
                            ins = turn(dst[:, t * P:(t + 1) * P], wrow[:, b * TH + t, :], idr)
                    elif w[0] == "spread":
                        h, e = w[1:]
                        pe.wait_ge(ring_taken, ring_no[("wrow", h)] + 1)
                        ins = mm(dst, select[:, e:e + 1].to_broadcast([P, P]), wT[:, h * HALF:(h + 1) * HALF],
                                 start=True, stop=True)
                    ins.then_inc(ring_filled, 1)
                elif kind == "scores":
                    b, p, u, j = w
                    n, c = unit_no(b, p, u), UNITS[u][j]
                    if n == 0 and j == 0:
                        pe.wait_ge(consts_ready, 4)
                        pe.wait_ge(v0_taken, CH)
                    if j == 0:
                        pe.wait_ge(ring_taken, ring_no[("shift", b, p)] + 1)
                        if n >= 2:
                            pe.wait_ge(probs_ready, n - 1)
                    rows = P if c < FULL else REST
                    ks = slice(c * P, c * P + rows)
                    dst = s_bank(n, j)[0:rows, :]
                    gh = g_hi[:, b % 2, 2 * p:2 * p + 2, :].rearrange("p h s -> p (h s)")
                    gl = g_lo[:, b % 2, 2 * p:2 * p + 2, :].rearrange("p h s -> p (h s)")
                    mm(dst, ctxT_hi[:, b % 2, ks], gh, start=True, stop=False)
                    mm(dst, ctxT_hi[0:C, b % 2, ks], gl, start=False, stop=False)
                    ins = mm(dst, ctxT_lo[:, b % 2, ks], gh[0:C], start=False, stop=True)
                    if c == UNITS[u][-1]:
                        ins.then_inc(scores_ready, 1)
                elif kind == "values":
                    b, p, u, j = w
                    n, pair, c = unit_no(b, p, u), b * PAIRS + p, UNITS[u][j]
                    if j == 0:
                        pe.wait_ge(probs_ready, n + 1)
                        if u == 0 and pair:
                            pe.wait_ge(o_raw_ready, pair)
                    rows = P if c < FULL else REST
                    if p == 0 and b:
                        pe.wait_ge(ring_taken, ring_no[("v", b, c)] + 1)
                    for i in range(2):
                        h = 2 * p + i
                        ins = mm(o_bank[DH * i:DH * (i + 1), :], v_sb[0:rows, c, h * DH:(h + 1) * DH],
                                 probs[0:rows, n % 4, j, i * S:(i + 1) * S], start=(c == 0), stop=(c == CH - 1))
                    if c == UNITS[u][-1]:
                        ins.then_inc(values_done, 1)
                elif kind == "v0":
                    c = w
                    rows = P if c < FULL else REST
                    pe.wait_ge(w_split, 1)
                    pe.wait_ge(ring_taken, ring_no[("turn", 0, c // 4)] + 1)
                    if c == 0:
                        pe.wait_ge(setup_taken, 3)
                    if c >= 4:
                        pe.wait_ge(v0_taken, c - 3)
                    ks = slice(c * P, c * P + rows)
                    three(ps[0:rows, c % 4, :], ctxT_hi[0:C, 0, ks], ctxT_lo[:, 0, ks], wv_hi[:], wv_lo[:]
                          ).then_inc(v0_filled, 1)
                elif kind == "first":
                    n, (h, e, k) = w, items[w]
                    if n == 0:
                        pe.wait_ge(probs_ready, LAST_UNIT)
                        pe.wait_ge(w_split, 3)
                    if n >= HB:
                        pe.wait_ge(hid_ready, n - HB + 1)
                    pe.wait_ge(ring_taken, ring_no[("xt", (h + 1) * B // NHALF - 1)] + 1)
                    q = slice(h * HALF, (h + 1) * HALF)
                    ks = slice(k * P, (k + 1) * P)
                    three(ps[:, n % HB, :], w1_hi[:, e, ks], w1_lo[:, e, ks], xnT_hi[:, q], xnT_lo[:, q]
                          ).then_inc(h_ready, 1)
                elif kind == "second":
                    n, (h, e, k) = w, items[w]
                    per = NI // NHALF
                    acc = out_bank(h)
                    if n % per == 0:
                        pe.wait_ge(o_raw_ready, B * PAIRS)
                        pe.wait_ge(s_b2, 48)
                        pe.wait_ge(w2_split, NE)
                        pe.wait_ge(ring_taken, ring_no[("wrow", h)] + 1)
                        mm(acc, b2_rows[:], wT[:, h * HALF:(h + 1) * HALF].bitcast(F32), start=True, stop=False)
                    pe.wait_ge(hid_lo_ready, n + 1)
                    three(acc, w2_hi[:, e, k, :], w2_lo(e)[:, k, :], hid_hi[:, n % SPLITS, :],
                          hid_lo[:, n % SPLITS, :], start=False, stop=(n % per == per - 1)).then_inc(w2_done, 1)
                elif kind == "back":
                    pe.wait_ge(outT_taken, w + 1)
                    for t in range(TH):
                        ins = turn(out_bank(w)[:, t * P:(t + 1) * P], outT[:, w, t * P:(t + 1) * P], idr)
                    ins.then_inc(back_filled, 1)


_INS = ["x", "ctx_768", "L0_xattn_Wq", "L0_xattn_Wk", "L0_xattn_Wv", "L0_xattn_Wo", "L0_xattn_bo",
        "L0_ffn_router_w", "L0_ffn_router_b", "L0_ffn_sw1", "L0_ffn_sb1", "L0_ffn_sw2", "L0_ffn_sb2",
        "L0_ffn_rw1", "L0_ffn_rb1", "L0_ffn_rw2", "L0_ffn_rb2"]


def kernel(**inputs):
    import numpy as _np
    import concourse.bacc as _bacc
    from concourse import mybir as _mybir
    from concourse.bass_utils import run_bass_kernel_spmd as _run

    nc = _bacc.Bacc("TRN2", target_bir_lowering=False, num_devices=1)
    arrays, args = {}, []
    for name in _INS:
        a = _np.ascontiguousarray(inputs[name])
        arrays[f"in_{name}_dram"] = a
        args.append(nc.dram_tensor(f"in_{name}_dram", a.shape, _mybir.dt.from_np(a.dtype), kind="ExternalInput").ap())
    shape = inputs["x"].shape
    out = nc.dram_tensor("out_0_dram", shape, _mybir.dt.from_np(_np.dtype("float32")), kind="ExternalOutput").ap()
    build(nc, *args, out)
    r = _run(nc, [arrays], core_ids=[0])
    return r.results[0]["out_0_dram"]
```
